# Optimizing a Trainium2 kernel written in Bass

```python
import numpy as np
import jax
import jax.numpy as jnp

def _softmax(x, axis=-1):
    return jax.nn.softmax(x, axis=axis)

def _gelu(x):
    return jax.nn.gelu(x, approximate=True)

def _silu(x):
    return jax.nn.silu(x)

def _sigmoid(x):
    return jax.nn.sigmoid(x)

def _layernorm(x, axis=-1, eps=1e-05):
    m = jnp.mean(x, axis=axis, keepdims=True)
    v = jnp.var(x, axis=axis, keepdims=True)
    return (x - m) / jnp.sqrt(v + eps)

def _scatter_add(tgt, idx, src, axis=0):
    return tgt.at[idx].add(src)

def _segment_sum(src, seg, n):
    return jax.ops.segment_sum(src, seg, n)
kernel_name = 'mk_prb_d1_jaxref_r8_55e2e9'

def setup_inputs(seed: int=0):
    np.random.seed(seed)
    _w = jnp.asarray

    def _L0_attn_setup():
        import jax, jax.numpy as jnp
        import numpy as np
        B, S, E, H = (2, 256, 128, 16)
        key = jax.random.key(seed)
        k0, k1, k2 = jax.random.split(key, 3)
        x = jax.random.normal(k0, (B, S, E), jnp.float32)
        w_in = jax.random.normal(k1, (3 * E, E), jnp.float32) / np.sqrt(E)
        b_in = jnp.zeros((3 * E,), jnp.float32)
        w_out = jax.random.normal(k2, (E, E), jnp.float32) / np.sqrt(E)
        b_out = jnp.zeros((E,), jnp.float32)
        return {'x': x, 'w_in': w_in, 'b_in': b_in, 'w_out': w_out, 'b_out': b_out}
    _L0_attn_in = _L0_attn_setup()

    def _L0_ffn_setup():
        import jax, jax.numpy as jnp
        import numpy as np
        B, S, D = (1, 256, 128)
        E, K, F = (8, 2, 176)
        NS = 2
        SCALE = 2.5

        def _swiglu_mlp(x, wg, wu, wd):
            return jax.nn.silu(x @ wg) * (x @ wu) @ wd
        key = jax.random.key(seed)
        ks = jax.random.split(key, 8)
        s = 0.02
        return {'hidden_states': jax.random.normal(ks[0], (B, S, D), jnp.float32), 'gate_w': jax.random.normal(ks[1], (E, D), jnp.float32) * s, 'w_gate': jax.random.normal(ks[2], (E, D, F), jnp.float32) * s, 'w_up': jax.random.normal(ks[3], (E, D, F), jnp.float32) * s, 'w_down': jax.random.normal(ks[4], (E, F, D), jnp.float32) * s, 'sw_gate': jax.random.normal(ks[5], (D, F * NS), jnp.float32) * s, 'sw_up': jax.random.normal(ks[6], (D, F * NS), jnp.float32) * s, 'sw_down': jax.random.normal(ks[7], (F * NS, D), jnp.float32) * s}
    _L0_ffn_in = _L0_ffn_setup()
    _d = {'L0_attn_x': _L0_attn_in['x'], 'L0_attn_w_in': _L0_attn_in['w_in'], 'L0_attn_b_in': _L0_attn_in['b_in'], 'L0_attn_w_out': _L0_attn_in['w_out'], 'L0_attn_b_out': _L0_attn_in['b_out'], 'L0_ffn_gate_w': _L0_ffn_in['gate_w'], 'L0_ffn_w_gate': _L0_ffn_in['w_gate'], 'L0_ffn_w_up': _L0_ffn_in['w_up'], 'L0_ffn_w_down': _L0_ffn_in['w_down'], 'L0_ffn_sw_gate': _L0_ffn_in['sw_gate'], 'L0_ffn_sw_up': _L0_ffn_in['sw_up'], 'L0_ffn_sw_down': _L0_ffn_in['sw_down']}
    _x0 = _d['L0_attn_x']
    _d['L0_attn_x'] = jax.random.normal(jax.random.fold_in(jax.random.key(seed), 1), (8, 512, 128), dtype=_x0.dtype)
    del _x0
    return _d

def reference(L0_attn_x, L0_attn_w_in, L0_attn_b_in, L0_attn_w_out, L0_attn_b_out, L0_ffn_gate_w, L0_ffn_w_gate, L0_ffn_w_up, L0_ffn_w_down, L0_ffn_sw_gate, L0_ffn_sw_up, L0_ffn_sw_down):

    def _L0_attn_ref(x, w_in, b_in, w_out, b_out):
        import jax, jax.numpy as jnp
        import numpy as np
        B, S, E, H = (2, 256, 128, 16)
        bsz, slen, esz = x.shape
        hsz = esz // H
        qkv = x @ w_in.T + b_in
        q, k, v = jnp.split(qkv, 3, axis=-1)

        def to_heads(t):
            return t.reshape(bsz, slen, H, hsz).transpose(0, 2, 1, 3)
        q, k, v = (to_heads(q), to_heads(k), to_heads(v))
        scale = np.float32(1.0 / np.sqrt(hsz))
        scores = jnp.einsum('bhqd,bhkd->bhqk', q * scale, k)
        causal_bias = jnp.where(jnp.tril(jnp.ones((slen, slen), dtype=bool)), 0.0, -jnp.inf).astype(x.dtype)
        scores = scores + causal_bias
        attn = jax.nn.softmax(scores, axis=-1)
        out = jnp.einsum('bhqk,bhkd->bhqd', attn, v)
        out = out.transpose(0, 2, 1, 3).reshape(bsz, slen, esz)
        out = out @ w_out.T + b_out
        out = jnp.where(jnp.isnan(out), jnp.zeros((), out.dtype), out)
        return out

    def _L0_ffn_ref(hidden_states, gate_w, w_gate, w_up, w_down, sw_gate, sw_up, sw_down):
        import jax, jax.numpy as jnp
        import numpy as np
        B, S, D = (1, 256, 128)
        E, K, F = (8, 2, 176)
        NS = 2
        SCALE = 2.5

        def _swiglu_mlp(x, wg, wu, wd):
            return jax.nn.silu(x @ wg) * (x @ wu) @ wd
        identity = hidden_states
        x = hidden_states.reshape(-1, hidden_states.shape[-1])
        T = x.shape[0]
        logits = x.astype(jnp.float32) @ gate_w.astype(jnp.float32).T
        scores = jax.nn.softmax(logits, axis=-1)
        topk_w, topk_i = jax.lax.top_k(scores, K)
        topk_w = topk_w / (topk_w.sum(-1, keepdims=True) + 1e-20) * SCALE
        combine = jnp.zeros((T, E), jnp.float32).at[jnp.arange(T)[:, None], topk_i].set(topk_w)
        g = jax.nn.silu(jnp.einsum('td,edf->etf', x, w_gate)) * jnp.einsum('td,edf->etf', x, w_up)
        expert_out = jnp.einsum('etf,efd->etd', g, w_down)
        y = jnp.einsum('te,etd->td', combine, expert_out).astype(x.dtype)
        y = y.reshape(identity.shape)
        return y + _swiglu_mlp(identity, sw_gate, sw_up, sw_down)
    x = L0_attn_x
    xn = _layernorm(x, axis=-1)
    x = x + _L0_attn_ref(xn, L0_attn_w_in, L0_attn_b_in, L0_attn_w_out, L0_attn_b_out) + _L0_ffn_ref(xn, L0_ffn_gate_w, L0_ffn_w_gate, L0_ffn_w_up, L0_ffn_w_down, L0_ffn_sw_gate, L0_ffn_sw_up, L0_ffn_sw_down)
    return x

_drawn_inputs = setup_inputs


def setup_inputs(seed=0):
    import zlib

    import numpy as np

    out = dict(_drawn_inputs(seed))
    spreads = {'L0_attn_b_in': (0.0, 0.1), 'L0_attn_b_out': (0.0, 0.285)}
    factors = {'L0_ffn_gate_w': 5.523,
     'L0_ffn_w_gate': 4.833,
     'L0_ffn_w_up': 4.804,
     'L0_ffn_w_down': 4.802,
     'L0_ffn_sw_gate': 6.064,
     'L0_ffn_sw_up': 6.06,
     'L0_ffn_sw_down': 6.06}
    for name, (base, spread) in spreads.items():
        noise = np.random.default_rng([zlib.crc32(name.encode()), seed]).standard_normal(out[name].shape)
        drawn = base * np.exp(spread * noise) if base else spread * noise
        out[name] = jnp.asarray(drawn.astype(out[name].dtype))
    for name, factor in factors.items():
        out[name] = (out[name] * factor).astype(out[name].dtype)
    return out
```

```python
from contextlib import ExitStack

import concourse.bass as bass
from concourse import mybir

F32 = mybir.dt.float32
F32R = mybir.dt.float32r
BF16 = mybir.dt.bfloat16
I32 = mybir.dt.int32
ALU = mybir.AluOpType
ACT = mybir.ActivationFunctionType
AX = mybir.AxisListType

P = 128
NB = 8
S = 512
QT = S // P
E = 128
H = 16
DH = E // H
PAIRS = H // 2
HALF = 64
GROUPS = H // 4
NE = 8
F = 176
FS = 352
FT = NE * F + FS
NT = -(-FT // P)
ROUTED = NE * F // P
LAST = FT - (NT - 1) * P
EPS = 1e-5
ROUTE_SCALE = 2.5
QSCALE = float(DH) ** -0.5
TERMS = 6
SROWS = TERMS * DH
MROWS = 3
TILE_ORDER = list(range(ROUTED, NT)) + list(range(ROUTED))
UNITS = 5
NAT = 10
EARLY = 2
PAIRS_AT = [(int(2 <= k <= 12), int(2 <= k <= 12 and k not in (2, 7))) for k in range(16)]
KB_ORDER = [0, 1, 3, 2]


def rows_of(tile):
    return LAST if tile == NT - 1 else P


def expert_segments():
    out = []
    for t in range(ROUTED):
        at = t * P
        while at < (t + 1) * P:
            e = at // F
            end = min((e + 1) * F, (t + 1) * P)
            out.append((t, at - t * P, end - at, e))
            at = end
    return out


def block_kernel(nc, x, wqkT, wvT, b_qk, b_v, woT, b_o, gateT, w_gu, w_dn, ident, halfid, halfmask, lower, out):
    ctx = ExitStack()
    with ctx:
        def sb(name, shape, dt=F32):
            return ctx.enter_context(nc.sbuf_tensor(name, shape, dt))

        def sem(name):
            return ctx.enter_context(nc.semaphore(name))

        x_sb = sb("x_sb", [P, NB * QT, E])
        wqk_sb = sb("wqk_sb", [P, 2, E])
        wv_sb = sb("wv_sb", [P, E])
        wo_sb = sb("wo_sb", [P, E])
        gate_sb = sb("gate_sb", [P, NE])
        bqk = sb("bqk", [P, 2])
        table_call = sb("table_call", [P, 1])
        bq_scaled = sb("bq_scaled", [P, 1])
        bv_bc = sb("bv_bc", [P, E])
        bo_bc = sb("bo_bc", [P, E])
        w_hi = sb("w_hi", [P, 2, FT], F32R)
        w_lo = sb("w_lo", [P, 2, FT], F32R)
        wd_sb = sb("wd_sb", [P, NT, E])
        ident_sb = sb("ident_sb", [P, P])
        ident_bf = sb("ident_bf", [P, P], BF16)
        halfid_f = sb("halfid_f", [P, 2, P])
        halfid_bf = sb("halfid_bf", [P, 2, P], BF16)
        mask_f = sb("mask_f", [P, 2, 2, P])
        mask_bf = sb("mask_bf", [P, 2, 2, P], BF16)
        lower_sb = sb("lower_sb", [P, NE, NE])
        stats = sb("stats", [P, NB * QT, 6])
        ln = sb("ln", [P, 8, NB * QT])
        xn = sb("xn", [P, QT, E])
        xnT = sb("xnT", [P, S])
        x_hi = sb("x_hi", [P, S], F32R)
        x_lo = sb("x_lo", [P, S], F32R)
        qk_f = sb("qk_f", [P, 2, S])
        qk_rest = sb("qk_rest", [P, 2, S])
        q_parts = sb("q_parts", [P, 3, S], BF16)
        k_parts = sb("k_parts", [P, 3, S], BF16)
        q_op = sb("q_op", [P, PAIRS, S], BF16)
        k_op = sb("k_op", [P, PAIRS, S], BF16)
        v_new = sb("v_new", [P, QT, E])
        v_op = sb("v_op", [P, QT, H, 32])
        neg_max = sb("neg_max", [P, QT, 2, PAIRS])
        max_rest = sb("max_rest", [P, QT, 2, PAIRS])
        max_parts = sb("max_parts", [P, QT, 3, 2, PAIRS], BF16)
        max_rows = sb("max_rows", [3 * H, S], BF16)
        probs = sb("probs", [P, 2, NAT, S])
        o_sb = sb("o_sb", [P, 2, S])
        o_rden = sb("o_rden", [P, QT, 4, 1])
        o_norm = sb("o_norm", [P, QT, E])
        o_normT = sb("o_normT", [P, S])
        rt = sb("rt", [P, 4, QT, NE])
        rt_pair = sb("rt_pair", [P, 2, QT, NE, NE])
        rt_s = sb("rt_s", [P, 5, QT])
        comb = sb("comb", [P, QT, NE])
        combT = sb("combT", [NE, S])
        cb = sb("cb", [P, ROUTED, S])
        sg = sb("sg", [P, 3, S])
        hid = sb("hid", [P, 3, S])
        yT = sb("yT", [P, S])
        base = sb("base", [P, QT, E])
        att = sb("att", [P, QT, E])
        both = sb("both", [P, QT, E])
        not_nan = sb("not_nan", [P, QT, E], I32)

        w_raw = probs[:, :, :, :].rearrange("p a b n -> p (a b n)")[:, 0:2 * FT].rearrange(
            "p (w f) -> p w f", w=2)

        ring = ctx.enter_context(nc.psum_tensor("ring", [P, 4, S], F32))
        nat = ctx.enter_context(nc.psum_tensor("nat", [P, 2, S], F32))
        bank_m = ctx.enter_context(nc.psum_tensor("bank_m", [P, S], F32))
        bank_y = ctx.enter_context(nc.psum_tensor("bank_y", [P, S], F32))

        q_dram = nc.dram_tensor("q_dram", [2, TERMS, DH, PAIRS, S], BF16, kind="Internal").ap()
        k_dram = nc.dram_tensor("k_dram", [2, TERMS, DH, PAIRS, S], BF16, kind="Internal").ap()
        m_dram = nc.dram_tensor("m_dram", [3, 2, PAIRS, S], BF16, kind="Internal").ap()
        c_dram = nc.dram_tensor("c_dram", [NE, S], F32, kind="Internal").ap()

        x_loaded = [sem(f"x_loaded{n}") for n in range(4)]
        w_loaded = sem("w_loaded")
        small_loaded = sem("small_loaded")
        ones_set = sem("ones_set")
        const_made = sem("const_made")
        wd_loaded = sem("wd_loaded")
        w_hi_done = sem("w_hi_done")
        w_lo_done = sem("w_lo_done")
        ln_step = sem("ln_step")
        sqrt_done = sem("sqrt_done")

        xn_done = sem("xn_done")
        xT_ready = sem("xT_ready")
        xnT_done = sem("xnT_done")
        xhl_step = sem("xhl_step")
        q_ready = sem("q_ready")
        k_ready = sem("k_ready")
        v_ready = sem("v_ready")
        q_done = sem("q_done")
        k_done = sem("k_done")
        v_done = sem("v_done")
        v_placed = sem("v_placed")
        qsplit_step = sem("qsplit_step")
        ksplit_step = sem("ksplit_step")
        q_written = sem("q_written")
        k_written = sem("k_written")
        ops_loaded = sem("ops_loaded")
        logits_ready = sem("logits_ready")
        router_exp = sem("router_exp")
        router_step = sem("router_step")
        combT_ready = sem("combT_ready")
        combT_done = sem("combT_done")
        comb_written = sem("comb_written")
        cb_loaded = sem("cb_loaded")
        cb_others = sem("cb_others")

        gate_ready = sem("gate_ready")
        up_ready = sem("up_ready")
        silu_done = sem("silu_done")
        weighted = sem("weighted")
        hid_done = sem("hid_done")
        down_done = sem("down_done")
        y_taken = sem("y_taken")
        yback_ready = sem("yback_ready")
        base_done = sem("base_done")

        nat_ready = sem("nat_ready")
        nat_max = sem("nat_max")
        msplit_step = sem("msplit_step")
        mT_ready = sem("mT_ready")
        mrows_done = sem("mrows_done")
        m_written = sem("m_written")
        m_loaded = sem("m_loaded")

        st_ready = sem("st_ready")
        exp_done = sem("exp_done")
        masked = sem("masked")
        pv_done = sem("pv_done")
        o_taken = sem("o_taken")
        oback_ready = sem("oback_ready")
        rden_done = sem("rden_done")
        o_normed = sem("o_normed")
        onT_ready = sem("onT_ready")
        onT_done = sem("onT_done")
        proj_ready = sem("proj_ready")
        tail_step = sem("tail_step")
        summed = sem("summed")
        stored = sem("stored")

        pe_passed = sem("pe_passed")
        dve_passed = sem("dve_passed")
        pool_passed = sem("pool_passed")
        sp_passed = sem("sp_passed")

        NAT_ALL = NAT * GROUPS
        ST_ALL = UNITS * GROUPS
        FIRST_SEGMENTS = [s for s in expert_segments() if s[0] < EARLY]
        OTHER_SEGMENTS = [s for s in expert_segments() if s[0] >= EARLY]
        OP_LOADS = 4
        PART_WRITES = 6
        ROUTER_STEPS = 15

        def half(h):
            return HALF * (h % 2)

        def apart(eng, counter):
            eng.sem_inc(counter, 1)

        def before(eng, s, count):
            if not (isinstance(count, int) and count == 0):
                eng.wait_ge(s, count)

        block = ctx.enter_context(nc.Block())

        @block.sync
        def _(sp):
            for n in range(4):
                k = NB * QT // 4
                sp.dma_start(x_sb[:, n * k:(n + 1) * k, :],
                             x.rearrange("b (q p) e -> p (b q) e", p=P)[:, n * k:(n + 1) * k, :]
                             ).then_inc(x_loaded[n], 16)
            sp.dma_start(w_raw, w_gu).then_inc(w_loaded, 16)
            small = [(ident_sb[:, :], ident), (wqk_sb[:, :, :], wqkT), (wv_sb[:, :], wvT),
                     (bqk[:, :], b_qk), (bv_bc[:, :], b_v.partition_broadcast(P)),
                     (gate_sb[:, :], gateT), (halfid_f[:, :, :], halfid),
                     (mask_f[:, :, 0, :], halfmask), (mask_f[:, :, 1, :], halfmask),
                     (lower_sb[:, :, :], lower.partition_broadcast(P)),
                     (wo_sb[:, :], woT), (bo_bc[:, :], b_o.partition_broadcast(P))]
            for dst, src in small:
                sp.dma_start(dst, src).then_inc(small_loaded, 16)
            sp.dma_start(wd_sb[:, 0:NT - 1, :], w_dn[0:(NT - 1) * P, :].rearrange("(t p) e -> p t e", p=P)
                         ).then_inc(wd_loaded, 16)
            sp.dma_start(wd_sb[0:LAST, NT - 1, :], w_dn[(NT - 1) * P:FT, :]).then_inc(wd_loaded, 16)

            def parts_out(j):
                sp.wait_ge(qsplit_step, 4 * j + 4)
                for s in range(2):
                    own = q_parts[HALF * s:HALF * (s + 1), :, :]
                    for first, n, part in ((0, 3, 0), (3, 2, 1), (5, 1, 2)):
                        sp.dma_start(q_dram[s, first:first + n].rearrange("t d i n -> (d i) t n"),
                                     own[:, part:part + 1, :].to_broadcast([HALF, n, S])
                                     ).then_inc(q_written, 16)
                sp.wait_ge(ksplit_step, 4 * j + 4)
                for s in range(2):
                    own = k_parts[HALF * s:HALF * (s + 1), :, :]
                    for first, n in ((0, 3), (3, 2), (5, 1)):
                        sp.dma_start(k_dram[s, first:first + n].rearrange("t d i n -> (d i) t n"),
                                     own[:, 0:n, :]).then_inc(k_written, 16)

            def weights_out(j):
                sp.wait_ge(combT_done, j + 1)
                sp.dma_start(c_dram, combT[:, :]).then_inc(comb_written, 16)
                sp.wait_ge(comb_written, 16 * j + 16)

            def weights_around(segments, loaded):
                for t, p0, n, e in segments:
                    sp.dma_start(cb[p0:p0 + n, t, :], c_dram[e, :].partition_broadcast(n)).then_inc(loaded, 16)

            def operands_in(j, i):
                if i is not None:
                    sp.wait_ge(st_ready, ST_ALL * i + ST_ALL)
                    apart(sp, sp_passed)
                sp.wait_ge(q_written, PART_WRITES * 16 * (j + 1))
                sp.wait_ge(k_written, PART_WRITES * 16 * (j + 1))
                for s in range(2):
                    rows = slice(HALF * s, HALF * s + SROWS)
                    sp.dma_start(q_op[rows, :, :], q_dram[s].rearrange("t d i n -> (t d) i n")
                                 ).then_inc(ops_loaded, 16)
                    sp.dma_start(k_op[rows, :, :], k_dram[s].rearrange("t d i n -> (t d) i n")
                                 ).then_inc(ops_loaded, 16)

            def store(i):
                sp.wait_ge(tail_step, 3 * i + 3)
                sp.dma_start(out[i].rearrange("(q p) e -> p q e", p=P), base[:, :, :]).then_inc(stored, 16)

            def maxima_in(b):
                sp.wait_ge(mrows_done, b + 1)
                before(sp, stored, 16 * b)
                sp.dma_start(m_dram.rearrange("a s i n -> (a s i) n"), max_rows[:, :]).then_inc(m_written, 16)
                sp.wait_ge(m_written, 16 * b + 16)
                for s in range(2):
                    row = HALF * s + SROWS
                    sp.dma_start(q_op[row:row + MROWS, :, :], m_dram[:, s, :, :]).then_inc(m_loaded, 16)

            parts_out(0)
            sp.wait_ge(ones_set, 1)
            operands_in(0, None)
            weights_out(0)
            weights_around(FIRST_SEGMENTS, cb_loaded)
            weights_around(OTHER_SEGMENTS, cb_others)
            maxima_in(0)
            with sp.Fori(0, NB - 1) as i:
                parts_out(i + 1)
                weights_out(i + 1)
                weights_around(FIRST_SEGMENTS, cb_loaded)
                operands_in(i + 1, i)
                weights_around(OTHER_SEGMENTS, cb_others)
                store(i)
                maxima_in(i + 1)
            store(NB - 1)
            sp.wait_ge(stored, 16 * NB)

        @block.tensor
        def _(pe):
            def transpose_x(j):
                pe.wait_ge(xn_done, j + 1)
                before(pe, y_taken, j)
                for q in range(QT):
                    mm = pe.transpose(bank_y[:, q * P:(q + 1) * P], xn[:, q, :], ident_sb[:, :])
                mm.then_inc(xT_ready, 1)

            def project_q(j):
                pe.wait_ge(xnT_done, j + 1)
                before(pe, base_done, j)
                pe.matmul(bank_m[:, :], wqk_sb[:, 0, :], xnT[:, :], start=True, stop=True).then_inc(q_ready, 1)

            def project_k(j):
                pe.wait_ge(xnT_done, j + 1)
                pe.matmul(bank_y[:, :], wqk_sb[:, 1, :], xnT[:, :], start=True, stop=True).then_inc(k_ready, 1)

            def project_v(j):
                pe.wait_ge(q_done, j + 1)
                for q in range(QT):
                    mm = pe.matmul(bank_m[:, q * P:(q + 1) * P], xnT[:, q * P:(q + 1) * P], wv_sb[:, :],
                                   start=True, stop=True)
                mm.then_inc(v_ready, 1)

            def logits(j):
                pe.wait_ge(k_done, j + 1)
                for q in range(QT):
                    mm = pe.matmul(bank_y[:, q * NE:(q + 1) * NE], xnT[:, q * P:(q + 1) * P], gate_sb[:, :],
                                   start=True, stop=True)
                mm.then_inc(logits_ready, 1)

            def transpose_comb(j):
                pe.wait_ge(router_step, ROUTER_STEPS * j + ROUTER_STEPS)
                pe.wait_ge(v_done, j + 1)
                for q in range(QT):
                    mm = pe.transpose(bank_m[0:NE, q * P:(q + 1) * P], comb[:, q, :], ident_sb[:, :])
                mm.then_inc(combT_ready, 1)

            def gate_up(b, k):
                tile = TILE_ORDER[k]
                n = rows_of(tile)
                if k == 0:
                    pe.wait_ge(xhl_step, 2 * b + 2)
                    before(pe, exp_done, ST_ALL * b)
                elif k >= 2:
                    pe.wait_ge(hid_done, NT * b + k - 1)
                for w, ready in ((0, gate_ready), (1, up_ready)):
                    bank = ring[0:n, 2 * (k % 2) + w, :]
                    cols = slice(tile * P, tile * P + n)
                    pe.matmul(bank, w_hi[:, w, cols], x_hi[:, :], start=True, stop=False)
                    pe.matmul(bank, w_hi[:, w, cols], x_lo[:, :], start=False, stop=False)
                    pe.matmul(bank, w_lo[:, w, cols], x_hi[:, :], start=False, stop=True).then_inc(ready, 1)

            def down(b, k, i):
                tile = TILE_ORDER[k]
                n = rows_of(tile)
                pe.wait_ge(hid_done, NT * b + k + 1)
                if k == 0:
                    pe.wait_ge(router_step, ROUTER_STEPS * b + 2)
                    if i is not None:
                        pe.wait_ge(o_normed, GROUPS * i + 3)
                pe.matmul(bank_y[:, :], wd_sb[0:n, tile, :], hid[0:n, k % 3, :],
                          start=(k == 0), stop=(k == NT - 1)).then_inc(down_done, 1)

            def mask_scores(bank, r, cols):
                c0, nblk, stride = cols
                for c in range(2):
                    w = P if c == 0 else HALF
                    if stride == P and nblk == 2 or nblk == 1:
                        o = bank[:, c0:c0 + nblk * P].rearrange("p (k n) -> p k n", k=nblk)[:, :, P - w:P]
                    else:
                        o = bank.rearrange("p (k n) -> p k n", n=stride)[:, :, c0:c0 + P][:, :, P - w:P]
                    mm = pe.matmul(o, halfid_bf[r:r + HALF, c, :], mask_bf[r:r + HALF, c, 0:nblk, P - w:P],
                                   start=False, stop=(c == 1), skip_group_check=True)
                return mm

            def scores(b, g, u):
                n = NAT * g + u
                bank = nat[:, n % 2, :]
                if n == 0:
                    pe.wait_ge(ops_loaded, OP_LOADS * 16 * b + OP_LOADS * 16)
                    before(pe, o_taken, GROUPS * b)
                elif n >= 2:
                    pe.wait_ge(nat_max, NAT_ALL * b + n - 1)
                if u < 8:
                    h = 4 * g + u % 4
                    r = half(h)
                    q = q_op[r:r + SROWS, h // 2, :]
                    k = k_op[r:r + SROWS, h // 2, :]
                    if u < 4:
                        pe.matmul(bank, q[:, 3 * P:4 * P], k, start=True, stop=False, skip_group_check=True)
                        mm = mask_scores(bank, r, (3 * P, 1, P))
                    else:
                        pe.matmul(bank[:, 0:3 * P], q[:, 2 * P:3 * P], k[:, 0:3 * P],
                                  start=True, stop=False, skip_group_check=True)
                        pe.matmul(bank[:, 3 * P:4 * P], q[:, 0:P], k[:, 0:P],
                                  start=False, stop=False, skip_group_check=True)
                        mm = mask_scores(bank, r, (2 * P, 2, P))
                else:
                    for n2, h in enumerate((4 * g + u - 8, 4 * g + u - 6)):
                        r = half(h)
                        pe.matmul(bank[:, n2 * 2 * P:(n2 + 1) * 2 * P], q_op[r:r + SROWS, h // 2, P:2 * P],
                                  k_op[r:r + SROWS, h // 2, 0:2 * P],
                                  start=(n2 == 0), stop=False, skip_group_check=True)
                    mm = mask_scores(bank, r, (P, 2, 2 * P))
                mm.then_inc(nat_ready, 1)

            def transpose_maxima(b):
                pe.wait_ge(msplit_step, 4 * b + 4)
                before(pe, tail_step, 3 * b)
                pe.wait_ge(combT_done, b + 1)
                apart(pe, pe_passed)
                rows = bank_m[0:3 * H, 0:S // 2].bitcast(BF16)
                for q in range(QT):
                    mm = pe.transpose(rows[:, q * P:(q + 1) * P],
                                      max_parts[:, q, :, :, :].rearrange("p a s i -> p (a s i)"), ident_bf[:, :])
                mm.then_inc(mT_ready, 1)

            def transpose_y(b):
                pe.wait_ge(y_taken, b + 1)
                pe.wait_ge(mrows_done, b + 1)
                for q in range(QT):
                    mm = pe.transpose(bank_m[:, q * P:(q + 1) * P], yT[:, q * P:(q + 1) * P], ident_sb[:, :])
                mm.then_inc(yback_ready, 1)

            def scores_t(i, g, u):
                n = UNITS * g + u
                if n == 0:
                    pe.wait_ge(m_loaded, 32 * i + 32)
                    pe.wait_ge(hid_done, NT * i + NT)
                elif n >= 2:
                    pe.wait_ge(exp_done, ST_ALL * i + n - 1)
                rows = SROWS + MROWS
                for a in range(2):
                    bank = ring[:, 2 * (n % 2) + a, :]
                    if u < 4:
                        h = 4 * g + 2 * (u % 2) + a
                        parts = [(h, 0, 0)] if u < 2 else [(h, 1, 0), (h, 3, 3 * P)]
                    else:
                        parts = [(4 * g + a, 2, 0), (4 * g + 2 + a, 2, 2 * P)]
                    for h, kb, at in parts:
                        r = half(h)
                        mm = pe.matmul(bank[:, at:at + S - kb * P],
                                       k_op[r:r + rows, h // 2, kb * P:(kb + 1) * P],
                                       q_op[r:r + rows, h // 2, kb * P:S], start=True, stop=True)
                mm.then_inc(st_ready, 1)

            def probs_of(g, j, kb):
                buf = probs[:, g % 2, :, :]
                if kb == 0:
                    return buf[:, j, :]
                if kb == 1:
                    return buf[:, 4 + j, 0:3 * P]
                if kb == 3:
                    return buf[:, 4 + j, 3 * P:4 * P]
                return buf[:, 8 + j % 2, (j // 2) * 2 * P:(j // 2 + 1) * 2 * P]

            def weigh_v(i, g, c):
                kb = KB_ORDER[c]
                pe.wait_ge(masked, 4 * GROUPS * i + 4 * g + c + 1)
                if c == 0:
                    if g == 0:
                        pe.wait_ge(v_placed, i + 1)
                    if g >= 2:
                        pe.wait_ge(o_taken, GROUPS * i + g - 1)
                for j in range(4):
                    mm = pe.matmul(nat[32 * j:32 * j + 32, g % 2, kb * P:S], v_op[:, kb, 4 * g + j, :],
                                   probs_of(g, j, kb), start=(c == 0), stop=(c == 3),
                                   tile_position=(0, 32 * j), skip_group_check=True)
                if c == 3:
                    mm.then_inc(pv_done, 1)

            def transpose_o(i, g, front):
                pe.wait_ge(o_taken, GROUPS * i + g + 1)
                bank = bank_y if g % 2 == 0 else bank_m
                if g == 0:
                    if front:
                        pe.wait_ge(router_step, ROUTER_STEPS * i + ROUTER_STEPS + 2)
                    else:
                        pe.wait_ge(y_taken, i + 1)
                elif g == 1:
                    if front:
                        pe.wait_ge(combT_done, i + 2)
                    else:
                        pe.wait_ge(base_done, i + 1)
                else:
                    pe.wait_ge(o_normed, GROUPS * i + g - 1)
                for q in range(QT):
                    mm = pe.transpose(bank[:, q * P:(q + 1) * P], o_sb[:, g % 2, q * P:(q + 1) * P],
                                      ident_sb[:, :])
                mm.then_inc(oback_ready, 1)

            def transpose_on(i):
                pe.wait_ge(o_normed, GROUPS * i + GROUPS)
                for q in range(QT):
                    mm = pe.transpose(bank_m[:, q * P:(q + 1) * P], o_norm[:, q, :], ident_sb[:, :])
                mm.then_inc(onT_ready, 1)

            def project_out(i):
                pe.wait_ge(onT_done, i + 1)
                for q in range(QT):
                    mm = pe.matmul(bank_m[:, q * P:(q + 1) * P], o_normT[:, q * P:(q + 1) * P], wo_sb[:, :],
                                   start=True, stop=True)
                mm.then_inc(proj_ready, 1)

            def experts_and_maxima(b, i):
                n = 0
                for k in range(NT + 2):
                    if k < NT:
                        gate_up(b, k)
                    if k == 0 and i is not None:
                        transpose_o(i, 3, True)
                    for part in range(2):
                        for _ in range(PAIRS_AT[k][part]):
                            scores(b, n // NAT, n % NAT)
                            scores(b, (n + 1) // NAT, (n + 1) % NAT)
                            n += 2
                        if part == 0 and k >= 2:
                            down(b, k - 2, i)
                    if k == 1 and i is not None:
                        transpose_on(i)
                    if k == 2 and i is not None:
                        project_out(i)
                    if k == 13:
                        transpose_maxima(b)

            def attend(i, front):
                if front:
                    transpose_x(i + 1)
                transpose_y(i)
                if front:
                    project_k(i + 1)
                    project_q(i + 1)
                for g in range(GROUPS + 1):
                    for u in range(UNITS):
                        if g < GROUPS:
                            scores_t(i, g, u)
                        if g > 0 and u < 4:
                            weigh_v(i, g - 1, u)
                        if u == 2 and g in (2, 3, 4):
                            transpose_o(i, g - 2, front)
                        if front:
                            if (g, u) == (0, 1):
                                logits(i + 1)
                            if (g, u) == (0, 3):
                                project_v(i + 1)
                            if (g, u) == (1, 4):
                                transpose_comb(i + 1)

            pe.wait_ge(small_loaded, 12 * 16)
            transpose_x(0)
            project_k(0)
            project_q(0)
            project_v(0)
            logits(0)
            transpose_comb(0)
            pe.wait_ge(const_made, 3)
            pe.wait_ge(w_lo_done, 2)
            pe.wait_ge(wd_loaded, 32)
            experts_and_maxima(0, None)
            with pe.Fori(0, NB - 1) as i:
                attend(i, True)
                experts_and_maxima(i + 1, i)
            attend(NB - 1, False)
            transpose_o(NB - 1, 3, False)
            transpose_on(NB - 1)
            project_out(NB - 1)

        @block.scalar
        def _(act):
            act.wait_ge(w_loaded, 16)
            for w in range(2):
                nc.scalar.activation(w_hi[:, w, :], w_raw[:, w, :], ACT.Copy).then_inc(w_hi_done, 1)
            act.wait_ge(ln_step, 7)
            nc.scalar.activation(ln[:, 5, :], ln[:, 4, :], ACT.Sqrt).then_inc(sqrt_done, 1)

            def take_xT(j):
                act.wait_ge(xT_ready, j + 1)
                nc.scalar.activation(xnT[:, :], bank_y[:, :], ACT.Copy).then_inc(xnT_done, 1)

            def take_q(j):
                act.wait_ge(q_ready, j + 1)
                nc.scalar.activation(qk_f[:, 0, :], bank_m[:, :], ACT.Identity, bias=bq_scaled[:, 0:1],
                                     scale=QSCALE).then_inc(q_done, 1)

            def take_k(j):
                act.wait_ge(k_ready, j + 1)
                nc.scalar.activation(qk_f[:, 1, :], bank_y[:, :], ACT.Identity, bias=bqk[:, 1:2],
                                     scale=1.0).then_inc(k_done, 1)

            def exp_router(j):
                act.wait_ge(router_step, ROUTER_STEPS * j + 2)
                nc.scalar.activation(rt[:, 1, :, :], rt[:, 0, :, :], ACT.Exp).then_inc(router_exp, 1)

            def silu(b, k):
                n = rows_of(TILE_ORDER[k])
                act.wait_ge(gate_ready, NT * b + k + 1)
                if k >= 3:
                    act.wait_ge(hid_done, NT * b + k - 2)
                else:
                    before(act, hid_done, NT * b)
                nc.scalar.activation(sg[0:n, k % 3, :], ring[0:n, 2 * (k % 2), :], ACT.Silu
                                     ).then_inc(silu_done, 1)

            def experts(b, i):
                for k in range(NT):
                    silu(b, k)
                    if k == 1 and i is not None:
                        act.wait_ge(onT_ready, i + 1)
                        nc.scalar.activation(o_normT[:, :], bank_m[:, :], ACT.Copy).then_inc(onT_done, 1)
                    if k == 13:
                        act.wait_ge(mT_ready, b + 1)
                        nc.scalar.activation(max_rows[:, :], bank_m[0:3 * H, 0:S // 2].bitcast(BF16), ACT.Copy
                                             ).then_inc(mrows_done, 1)
                act.wait_ge(down_done, NT * b + NT)
                nc.scalar.activation(yT[:, :], bank_y[:, :], ACT.Copy).then_inc(y_taken, 1)
                nc.scalar.activation(table_call[:, :], bqk[:, 1:2], ACT.Exp)

            def attend(i, front):
                if front:
                    take_xT(i + 1)
                    take_k(i + 1)
                    take_q(i + 1)
                for g in range(GROUPS):
                    for u in range(UNITS):
                        n = UNITS * g + u
                        act.wait_ge(st_ready, ST_ALL * i + n + 1)
                        if u == 0 and g >= 2:
                            act.wait_ge(pv_done, GROUPS * i + g - 1)
                        nc.scalar.activation(probs[:, g % 2, 2 * u:2 * u + 2, :],
                                             ring[:, 2 * (n % 2):2 * (n % 2) + 2, :], ACT.Exp
                                             ).then_inc(exp_done, 1)
                        if front:
                            if (g, u) == (0, 3):
                                exp_router(i + 1)

            take_xT(0)
            act.wait_ge(const_made, 4)
            take_k(0)
            take_q(0)
            exp_router(0)
            act.wait_ge(w_lo_done, 2)
            experts(0, None)
            with act.Fori(0, NB - 1) as i:
                attend(i, True)
                experts(i + 1, i)
            attend(NB - 1, False)
            act.wait_ge(onT_ready, NB)
            nc.scalar.activation(o_normT[:, :], bank_m[:, :], ACT.Copy).then_inc(onT_done, 1)

        @block.gpsimd
        def _(pool):
            nc.gpsimd.memset(k_op[:, :, :], 1.0).then_inc(ones_set, 1)
            nc.gpsimd.memset(v_op[:, :, :, DH + 1:32], 0.0)
            nc.gpsimd.memset(v_op[:, :, :, DH:DH + 1], 1.0)

            def place_v(j, i):
                pool.wait_ge(v_done, j + 1)
                if i is not None:
                    pool.wait_ge(pv_done, GROUPS * i + GROUPS)
                apart(pool, pool_passed)
                nc.gpsimd.tensor_copy(v_op[:, :, :, 0:DH], v_new[:, :, :].rearrange(
                    "p q (h d) -> p q h d", h=H)).then_inc(v_placed, 1)

            def weigh_hidden(b, k):
                pool.wait_ge(silu_done, NT * b + k + 1)
                nc.gpsimd.tensor_tensor(sg[:, k % 3, :], sg[:, k % 3, :], cb[:, TILE_ORDER[k], :], ALU.mult
                                        ).then_inc(weighted, 1)

            def experts(b, i):
                pool.wait_ge(cb_loaded, 16 * len(FIRST_SEGMENTS) * (b + 1))
                for k in range(NT - ROUTED, NT):
                    if k == NT - ROUTED + 1 and i is not None:
                        sum_all(i)
                    if k == NT - ROUTED + EARLY:
                        pool.wait_ge(cb_others, 16 * len(OTHER_SEGMENTS) * (b + 1))
                    weigh_hidden(b, k)

            def sum_all(i):
                pool.wait_ge(tail_step, 3 * i + 1)
                nc.gpsimd.tensor_tensor(both[:, :, :], att[:, :, :], base[:, :, :], ALU.add).then_inc(summed, 1)

            def mask(view):
                apart(pool, pool_passed)
                return nc.gpsimd.affine_select(out=view, in_=view, compare_op=ALU.is_ge, fill=0.0, base=0,
                                               pattern=[[0, 4], [1, P]], channel_multiplier=-1)

            def attend(i, front):
                for g in range(GROUPS):
                    buf = probs[:, g % 2, :, :]
                    first = ST_ALL * i + UNITS * g
                    pool.wait_ge(exp_done, first + 2)
                    mask(buf[:, 0:4, 0:P]).then_inc(masked, 1)
                    pool.wait_ge(exp_done, first + 4)
                    mask(buf[:, 4:8, 0:P]).then_inc(masked, 1)
                    mask(buf[:, 4:8, 3 * P:4 * P]).then_inc(masked, 1)
                    pool.wait_ge(exp_done, first + 5)
                    mask(buf[:, 8:10, :].rearrange("p b (j n) -> p (b j) n", j=2)[:, :, 0:P]
                         ).then_inc(masked, 1)
                if front:
                    place_v(i + 1, i)

            for w in range(2):
                pool.wait_ge(w_hi_done, w + 1)
                nc.gpsimd.tensor_tensor(w_lo[:, w, :], w_raw[:, w, :], w_hi[:, w, :].bitcast(F32),
                                        ALU.subtract).then_inc(w_lo_done, 1)
            place_v(0, None)
            experts(0, None)
            with pool.Fori(0, NB - 1) as i:
                attend(i, True)
                experts(i + 1, i)
            attend(NB - 1, False)
            sum_all(NB - 1)

        @block.vector
        def _(dve):
            TT = NB * QT
            for t in range(TT):
                if t % (TT // 4) == 0:
                    dve.wait_ge(x_loaded[t // (TT // 4)], 16)
                last = nc.vector.bn_stats(stats[:, t, :], x_sb[:, t, :])
            last.then_inc(ln_step, 1)
            dve.wait_ge(ln_step, 1)
            nc.vector.tensor_tensor(ln[:, 0, :], stats[:, :, 1], stats[:, :, 4], ALU.add)
            nc.vector.tensor_tensor(ln[:, 1, :], stats[:, :, 1], stats[:, :, 4], ALU.subtract).then_inc(ln_step, 1)
            dve.wait_ge(ln_step, 2)
            nc.vector.tensor_tensor(ln[:, 2, :], stats[:, :, 2], stats[:, :, 5], ALU.add).then_inc(ln_step, 1)
            nc.vector.scalar_tensor_tensor(out=ln[:, 3, :], in0=ln[:, 1, :], scalar=0.25, in1=ln[:, 1, :],
                                           op0=ALU.mult, op1=ALU.mult).then_inc(ln_step, 1)
            dve.wait_ge(ln_step, 4)
            nc.vector.tensor_scalar(ln[:, 2, :], ln[:, 2, :], 1.0 / E, EPS, ALU.mult, ALU.add).then_inc(ln_step, 1)
            dve.wait_ge(ln_step, 5)
            nc.vector.tensor_tensor(ln[:, 4, :], ln[:, 2, :], ln[:, 3, :], ALU.add).then_inc(ln_step, 1)
            nc.vector.tensor_scalar(ln[:, 0, :], ln[:, 0, :], 0.5, None, ALU.mult).then_inc(ln_step, 1)
            dve.wait_ge(sqrt_done, 1)
            nc.vector.reciprocal(ln[:, 6, :], ln[:, 5, :]).then_inc(ln_step, 1)
            dve.wait_ge(ln_step, 8)
            nc.vector.tensor_tensor(ln[:, 7, :], ln[:, 6, :], ln[:, 6, :], ALU.mult).then_inc(ln_step, 1)
            dve.wait_ge(ln_step, 9)
            nc.vector.tensor_tensor(ln[:, 7, :], ln[:, 7, :], ln[:, 4, :], ALU.mult).then_inc(ln_step, 1)
            dve.wait_ge(ln_step, 10)
            nc.vector.tensor_scalar(ln[:, 7, :], ln[:, 7, :], -0.5, 1.5, ALU.mult, ALU.add).then_inc(ln_step, 1)
            dve.wait_ge(ln_step, 11)
            nc.vector.tensor_tensor(ln[:, 6, :], ln[:, 6, :], ln[:, 7, :], ALU.mult).then_inc(ln_step, 1)
            dve.wait_ge(ln_step, 12)

            def normalise(j):
                before(dve, xT_ready, j)
                for q in range(QT):
                    at = bass.ds(j * QT + q, 1)
                    last = nc.vector.tensor_scalar(xn[:, q, :], x_sb[:, at, :].rearrange("p t e -> p (t e)"),
                                                   ln[:, 0, at], ln[:, 6, at], ALU.subtract, ALU.mult)
                last.then_inc(xn_done, 1)

            def split_x(j):
                dve.wait_ge(xnT_done, j + 1)
                if not (isinstance(j, int) and j == 0):
                    dve.wait_ge(up_ready, NT * j)
                nc.vector.tensor_copy(x_hi[:, :], xnT[:, :]).then_inc(xhl_step, 1)
                dve.wait_ge(xhl_step, 2 * j + 1)
                nc.vector.tensor_tensor(x_lo[:, :], xnT[:, :], x_hi[:, :].bitcast(F32), ALU.subtract
                                        ).then_inc(xhl_step, 1)

            def split_qk(j, n, taken, parts, step, written):
                whole, rest = qk_f[:, n, :], qk_rest[:, n, :]
                dve.wait_ge(taken, j + 1)
                before(dve, written, PART_WRITES * 16 * j)
                nc.vector.tensor_copy(parts[:, 0, :], whole).then_inc(step, 1)
                dve.wait_ge(step, 4 * j + 1)
                nc.vector.tensor_tensor(rest, whole, parts[:, 0, :], ALU.subtract).then_inc(step, 1)
                dve.wait_ge(step, 4 * j + 2)
                nc.vector.tensor_copy(parts[:, 1, :], rest).then_inc(step, 1)
                dve.wait_ge(step, 4 * j + 3)
                nc.vector.tensor_tensor(parts[:, 2, :], rest, parts[:, 1, :], ALU.subtract).then_inc(step, 1)

            def split_q(j):
                split_qk(j, 0, q_done, q_parts, qsplit_step, q_written)

            def split_k(j):
                split_qk(j, 1, k_done, k_parts, ksplit_step, k_written)

            def take_v(j):
                dve.wait_ge(v_ready, j + 1)
                before(dve, v_placed, j)
                nc.vector.tensor_tensor(v_new[:, :, :], bank_m[:, :].rearrange("p (q e) -> p q e", q=QT),
                                        bv_bc[:, :].unsqueeze(1).to_broadcast([P, QT, E]), ALU.add
                                        ).then_inc(v_done, 1)

            def wide(ap):
                return ap.unsqueeze(2).to_broadcast([P, QT, NE])

            def router_logits(j):
                lg = bank_y[:, 0:QT * NE].rearrange("p (q e) -> p q e", q=QT)
                dve.wait_ge(logits_ready, j + 1)
                nc.vector.reduce_max(rt_s[:, 0, :], lg, AX.X).then_inc(router_step, 1)
                dve.wait_ge(router_step, ROUTER_STEPS * j + 1)
                nc.vector.tensor_tensor(rt[:, 0, :, :], lg, wide(rt_s[:, 0, :]), ALU.subtract
                                        ).then_inc(router_step, 1)

            def router_weights(j):
                n = [2]

                def then(ins):
                    n[0] += 1
                    ins.then_inc(router_step, 1)
                    dve.wait_ge(router_step, ROUTER_STEPS * j + n[0])

                v = nc.vector
                score = rt[:, 2, :, :]
                of_e = score.unsqueeze(3).to_broadcast([P, QT, NE, NE])
                of_o = score.unsqueeze(2).to_broadcast([P, QT, NE, NE])
                above, ties = rt_pair[:, 0, :, :, :], rt_pair[:, 1, :, :, :]
                dve.wait_ge(router_exp, j + 1)
                then(v.reduce_sum(rt_s[:, 1, :], rt[:, 1, :, :], AX.X))
                then(v.reciprocal(rt_s[:, 1, :], rt_s[:, 1, :]))
                then(v.tensor_tensor(score, rt[:, 1, :, :], wide(rt_s[:, 1, :]), ALU.mult))
                then(v.tensor_tensor(ties, of_o, of_e, ALU.is_equal))
                then(v.tensor_tensor(ties, ties, lower_sb[:, :, :].unsqueeze(1).to_broadcast([P, QT, NE, NE]),
                                     ALU.mult))
                then(v.tensor_tensor(above, of_o, of_e, ALU.is_gt))
                then(v.tensor_tensor(above, above, ties, ALU.add))
                then(v.reduce_sum(rt[:, 3, :, :], above, AX.X))
                then(v.scalar_tensor_tensor(out=rt[:, 3, :, :], in0=rt[:, 3, :, :], scalar=1.5, in1=score,
                                            op0=ALU.is_lt, op1=ALU.mult))
                then(v.reduce_sum(rt_s[:, 2, :], rt[:, 3, :, :], AX.X))
                then(v.tensor_scalar(rt_s[:, 3, :], rt_s[:, 2, :], 1e-20, None, ALU.add))
                then(v.reciprocal(rt_s[:, 4, :], rt_s[:, 3, :]))
                then(v.scalar_tensor_tensor(out=comb[:, :, :], in0=rt[:, 3, :, :], scalar=ROUTE_SCALE,
                                            in1=wide(rt_s[:, 4, :]), op0=ALU.mult, op1=ALU.mult))
                assert n[0] == ROUTER_STEPS

            def take_combT(j):
                dve.wait_ge(combT_ready, j + 1)
                before(dve, comb_written, 16 * j)
                nc.vector.tensor_copy(combT[:, :], bank_m[0:NE, :]).then_inc(combT_done, 1)

            def hidden(b, k):
                n = rows_of(TILE_ORDER[k])
                shared = NT - ROUTED
                if k < shared:
                    dve.wait_ge(silu_done, NT * b + k + 1)
                else:
                    dve.wait_ge(weighted, ROUTED * b + k - shared + 1)
                dve.wait_ge(up_ready, NT * b + k + 1)
                before(dve, down_done, NT * b + (k - 2 if k >= 3 else 0))
                nc.vector.tensor_tensor(hid[0:n, k % 3, :], sg[0:n, k % 3, :], ring[0:n, 2 * (k % 2) + 1, :],
                                        ALU.mult).then_inc(hid_done, 1)

            def maxima(b, g, u):
                n = NAT * g + u
                bank = nat[:, n % 2, :]
                dve.wait_ge(nat_ready, NAT_ALL * b + n + 1)
                def neg(out, in_):
                    return nc.vector.tensor_reduce(out, in_, AX.X, ALU.max, negate=True)

                if u < 8:
                    h = 4 * g + u % 4
                    s, i = h % 2, h // 2
                if u < 4:
                    last = neg(neg_max[:, 3, s, i:i + 1], bank)
                elif u < 8:
                    neg(neg_max[:, 2, s, i:i + 1], bank[:, 0:3 * P])
                    last = neg(neg_max[:, 0, s, i:i + 1], bank[:, 3 * P:4 * P])
                else:
                    last = neg(neg_max[:, 1, u - 8, 2 * g:2 * g + 2], bank.rearrange("p (k n) -> p k n", k=2))
                last.then_inc(nat_max, 1)

            def split_maxima(b):
                dve.wait_ge(nat_max, NAT_ALL * b + NAT_ALL)
                before(dve, mT_ready, b)
                nc.vector.tensor_copy(max_parts[:, :, 0, :, :], neg_max[:, :, :, :]).then_inc(msplit_step, 1)
                dve.wait_ge(msplit_step, 4 * b + 1)
                nc.vector.tensor_tensor(max_rest[:, :, :, :], neg_max[:, :, :, :], max_parts[:, :, 0, :, :],
                                        ALU.subtract).then_inc(msplit_step, 1)
                dve.wait_ge(msplit_step, 4 * b + 2)
                nc.vector.tensor_copy(max_parts[:, :, 1, :, :], max_rest[:, :, :, :]).then_inc(msplit_step, 1)
                dve.wait_ge(msplit_step, 4 * b + 3)
                nc.vector.tensor_tensor(max_parts[:, :, 2, :, :], max_rest[:, :, :, :],
                                        max_parts[:, :, 1, :, :], ALU.subtract).then_inc(msplit_step, 1)

            def take_o(i, g):
                dve.wait_ge(pv_done, GROUPS * i + g + 1)
                if g >= 2:
                    dve.wait_ge(oback_ready, GROUPS * i + g - 1)
                nc.vector.tensor_copy(o_sb[:, g % 2, :], nat[:, g % 2, :]).then_inc(o_taken, 1)

            def normalise_o(i, g):
                bank = (bank_y if g % 2 == 0 else bank_m)[:, :].rearrange("p (q j c) -> p q j c", q=QT, j=4)
                dve.wait_ge(oback_ready, GROUPS * i + g + 1)
                nc.vector.reciprocal(o_rden[:, :, :, :], bank[:, :, :, DH:DH + 1]).then_inc(rden_done, 1)
                dve.wait_ge(rden_done, GROUPS * i + g + 1)
                nc.vector.tensor_tensor(
                    o_norm[:, :, 4 * DH * g:4 * DH * (g + 1)].rearrange("p q (j d) -> p q j d", j=4),
                    bank[:, :, :, 0:DH], o_rden[:, :, :, :].to_broadcast([P, QT, 4, DH]), ALU.mult
                ).then_inc(o_normed, 1)

            def add_tokens(b):
                dve.wait_ge(m_written, 16 * b + 16)
                dve.wait_ge(yback_ready, b + 1)
                nc.vector.tensor_tensor(base[:, :, :], bank_m[:, :].rearrange("p (q e) -> p q e", q=QT),
                                        x_sb[:, bass.ds(b * QT, QT), :], ALU.add).then_inc(base_done, 1)

            def add_attention(i):
                dve.wait_ge(proj_ready, i + 1)
                nc.vector.tensor_tensor(att[:, :, :], bank_m[:, :].rearrange("p (q e) -> p q e", q=QT),
                                        bo_bc[:, :].unsqueeze(1).to_broadcast([P, QT, E]), ALU.add
                                        ).then_inc(tail_step, 1)

            def find_numbers(i):
                dve.wait_ge(tail_step, 3 * i + 1)
                nc.vector.tensor_tensor(not_nan[:, :, :], att[:, :, :], att[:, :, :], ALU.is_equal
                                        ).then_inc(tail_step, 1)

            def finish_output(i):
                dve.wait_ge(tail_step, 3 * i + 2)
                apart(dve, dve_passed)
                dve.wait_ge(summed, i + 1)
                apart(dve, dve_passed)
                apart(dve, dve_passed)
                nc.vector.copy_predicated(base[:, :, :], not_nan[:, :, :], both[:, :, :]).then_inc(tail_step, 1)

            def experts_and_maxima(b, i):
                if i is not None:
                    take_o(i, 3)
                n = 0
                for k in range(NT + 1):
                    if k == 1 and i is not None:
                        normalise_o(i, 3)
                    if k >= 1:
                        hidden(b, k - 1)
                    for _ in range(sum(PAIRS_AT[k])):
                        maxima(b, n // NAT, n % NAT)
                        maxima(b, (n + 1) // NAT, (n + 1) % NAT)
                        n += 2
                    if k == 12:
                        split_maxima(b)
                    if k == 3 and i is not None:
                        add_attention(i)
                    if k == 5 and i is not None:
                        find_numbers(i)
                    if k == 7 and i is not None:
                        finish_output(i)

            def attend(i, front):
                if front:
                    normalise(i + 1)
                add_tokens(i)
                if front:
                    split_k(i + 1)
                    router_logits(i + 1)
                    take_v(i + 1)
                    split_q(i + 1)
                    router_weights(i + 1)
                take_o(i, 0)
                normalise_o(i, 0)
                if front:
                    take_combT(i + 1)
                take_o(i, 1)
                if front:
                    split_x(i + 1)
                normalise_o(i, 1)
                take_o(i, 2)
                normalise_o(i, 2)

            normalise(0)
            dve.wait_ge(small_loaded, 12 * 16)
            nc.vector.tensor_copy(ident_bf[:, :], ident_sb[:, :]).then_inc(const_made, 1)
            nc.vector.tensor_copy(halfid_bf[:, :, :], halfid_f[:, :, :]).then_inc(const_made, 1)
            nc.vector.tensor_copy(mask_bf[:, :, :, :], mask_f[:, :, :, :]).then_inc(const_made, 1)
            nc.vector.tensor_scalar(bq_scaled[:, :], bqk[:, 0:1], QSCALE, None, ALU.mult).then_inc(const_made, 1)
            split_x(0)
            split_k(0)
            split_q(0)
            router_logits(0)
            take_v(0)
            router_weights(0)
            take_combT(0)
            experts_and_maxima(0, None)
            with dve.Fori(0, NB - 1) as i:
                attend(i, True)
                experts_and_maxima(i + 1, i)
            attend(NB - 1, False)
            take_o(NB - 1, 3)
            normalise_o(NB - 1, 3)
            add_attention(NB - 1)
            find_numbers(NB - 1)
            finish_output(NB - 1)


def kernel(L0_attn_x, L0_attn_w_in, L0_attn_b_in, L0_attn_w_out, L0_attn_b_out, L0_ffn_gate_w, L0_ffn_w_gate,
           L0_ffn_w_up, L0_ffn_w_down, L0_ffn_sw_gate, L0_ffn_sw_up, L0_ffn_sw_down):
    import numpy as np
    import concourse.bacc as bacc
    from concourse.bass_utils import run_bass_kernel_spmd

    def side_by_side(w, sw):
        return np.concatenate([np.transpose(w, (1, 0, 2)).reshape(E, NE * F), sw], axis=1)

    r = np.arange(P)
    halfid = np.zeros((P, 2, P), np.float32)
    halfmask = np.zeros((P, 2, P), np.float32)
    for c in range(2):
        q = HALF * c + r % HALF
        halfid[r, c, q] = 1.0
        halfmask[:, c, :] = np.where(r[None, :] > q[:, None], np.float32(-3e38), np.float32(0))
    lower = (np.arange(NE)[None, :] < np.arange(NE)[:, None]).astype(np.float32)

    w_in = np.asarray(L0_attn_w_in)
    b_in = np.asarray(L0_attn_b_in)
    ins = {
        "x": np.asarray(L0_attn_x),
        "wqkT": np.transpose(w_in[:2 * E].reshape(2, PAIRS, 2, DH, E), (4, 0, 2, 3, 1)).reshape(E, 2, E),
        "wvT": w_in[2 * E:].T,
        "b_qk": np.transpose(b_in[:2 * E].reshape(2, PAIRS, 2, DH), (2, 3, 1, 0)).reshape(E, 2),
        "b_v": b_in[2 * E:],
        "woT": np.asarray(L0_attn_w_out).T,
        "b_o": np.asarray(L0_attn_b_out),
        "gateT": np.asarray(L0_ffn_gate_w).T,
        "w_gu": np.stack([side_by_side(np.asarray(L0_ffn_w_gate), np.asarray(L0_ffn_sw_gate)),
                          side_by_side(np.asarray(L0_ffn_w_up), np.asarray(L0_ffn_sw_up))], axis=1),
        "w_dn": np.concatenate([np.asarray(L0_ffn_w_down).reshape(NE * F, E), np.asarray(L0_ffn_sw_down)]),
        "ident": np.eye(P, dtype=np.float32),
        "halfid": halfid,
        "halfmask": halfmask,
        "lower": lower,
    }
    nc = bacc.Bacc("TRN2", target_bir_lowering=False, num_devices=1)
    arrays, aps = {}, []
    for name, a in ins.items():
        a = np.ascontiguousarray(a)
        arrays[f"in_{name}"] = a
        aps.append(nc.dram_tensor(f"in_{name}", a.shape, mybir.dt.from_np(a.dtype), kind="ExternalInput").ap())
    out = nc.dram_tensor("out_0", (NB, S, E), F32, kind="ExternalOutput").ap()
    block_kernel(nc, *aps, out)
    res = run_bass_kernel_spmd(nc, [arrays], core_ids=[0])
    return res.results[0]["out_0"]
```

```python
from contextlib import ExitStack

import concourse.bass as bass
from concourse import mybir

F32 = mybir.dt.float32
F32R = mybir.dt.float32r
BF16 = mybir.dt.bfloat16
I32 = mybir.dt.int32
ALU = mybir.AluOpType
ACT = mybir.ActivationFunctionType
AX = mybir.AxisListType

P = 128
NB = 8
S = 512
QT = S // P
E = 128
H = 16
DH = E // H
PAIRS = H // 2
HALF = 64
GROUPS = H // 4
NE = 8
F = 176
FS = 352
FT = NE * F + FS
NT = -(-FT // P)
ROUTED = NE * F // P
LAST = FT - (NT - 1) * P
EPS = 1e-5
ROUTE_SCALE = 2.5
QSCALE = float(DH) ** -0.5
TERMS = 6
SROWS = TERMS * DH
MROWS = 3
TILE_ORDER = list(range(ROUTED, NT)) + list(range(ROUTED))
UNITS = 5
NAT = 10
EARLY = 2
PAIRS_AT = [(int(2 <= k <= 12), int(2 <= k <= 12 and k not in (2, 7))) for k in range(16)]
KB_ORDER = [0, 1, 3, 2]


def rows_of(tile):
    return LAST if tile == NT - 1 else P


def expert_segments():
    out = []
    for t in range(ROUTED):
        at = t * P
        while at < (t + 1) * P:
            e = at // F
            end = min((e + 1) * F, (t + 1) * P)
            out.append((t, at - t * P, end - at, e))
            at = end
    return out


def block_kernel(nc, x, wqkT, wvT, b_qk, b_v, woT, b_o, gateT, w_gu, w_dn, ident, halfid, halfmask, lower, out):
    ctx = ExitStack()
    with ctx:
        def sb(name, shape, dt=F32):
            return ctx.enter_context(nc.sbuf_tensor(name, shape, dt))

        def sem(name):
            return ctx.enter_context(nc.semaphore(name))

        x_sb = sb("x_sb", [P, NB * QT, E])
        wqk_sb = sb("wqk_sb", [P, 2, E])
        wv_sb = sb("wv_sb", [P, E])
        wo_sb = sb("wo_sb", [P, E])
        gate_sb = sb("gate_sb", [P, NE])
        bqk = sb("bqk", [P, 2])
        table_call = sb("table_call", [P, 1])
        bq_scaled = sb("bq_scaled", [P, 1])
        bv_bc = sb("bv_bc", [P, E])
        bo_bc = sb("bo_bc", [P, E])
        w_hi = sb("w_hi", [P, 2, FT], F32R)
        w_lo = sb("w_lo", [P, 2, FT], F32R)
        wd_sb = sb("wd_sb", [P, NT, E])
        ident_sb = sb("ident_sb", [P, P])
        ident_bf = sb("ident_bf", [P, P], BF16)
        halfid_f = sb("halfid_f", [P, 2, P])
        halfid_bf = sb("halfid_bf", [P, 2, P], BF16)
        mask_f = sb("mask_f", [P, 2, 2, P])
        mask_bf = sb("mask_bf", [P, 2, 2, P], BF16)
        lower_sb = sb("lower_sb", [P, NE, NE])
        stats = sb("stats", [P, NB * QT, 6])
        ln = sb("ln", [P, 8, NB * QT])
        xn = sb("xn", [P, QT, E])
        xnT = sb("xnT", [P, S])
        x_hi = sb("x_hi", [P, S], F32R)
        x_lo = sb("x_lo", [P, S], F32R)
        qk_f = sb("qk_f", [P, 2, S])
        qk_rest = sb("qk_rest", [P, 2, S])
        q_parts = sb("q_parts", [P, 3, S], BF16)
        k_parts = sb("k_parts", [P, 3, S], BF16)
        q_op = sb("q_op", [P, PAIRS, S], BF16)
        k_op = sb("k_op", [P, PAIRS, S], BF16)
        v_new = sb("v_new", [P, QT, E])
        v_op = sb("v_op", [P, QT, H, 32])
        neg_max = sb("neg_max", [P, QT, 2, PAIRS])
        max_rest = sb("max_rest", [P, QT, 2, PAIRS])
        max_parts = sb("max_parts", [P, QT, 3, 2, PAIRS], BF16)
        max_rows = sb("max_rows", [3 * H, S], BF16)
        probs = sb("probs", [P, 2, NAT, S])
        o_sb = sb("o_sb", [P, 2, S])
        o_rden = sb("o_rden", [P, QT, 4, 1])
        o_norm = sb("o_norm", [P, QT, E])
        o_normT = sb("o_normT", [P, S])
        rt = sb("rt", [P, 4, QT, NE])
        rt_pair = sb("rt_pair", [P, 2, QT, NE, NE])
        rt_s = sb("rt_s", [P, 5, QT])
        comb = sb("comb", [P, QT, NE])
        combT = sb("combT", [NE, S])
        cb = sb("cb", [P, ROUTED, S])
        sg = sb("sg", [P, 3, S])
        hid = sb("hid", [P, 3, S])
        yT = sb("yT", [P, S])
        base = sb("base", [P, QT, E])
        att = sb("att", [P, QT, E])
        both = sb("both", [P, QT, E])
        not_nan = sb("not_nan", [P, QT, E], I32)

        w_raw = probs[:, :, :, :].rearrange("p a b n -> p (a b n)")[:, 0:2 * FT].rearrange(
            "p (w f) -> p w f", w=2)

        ring = ctx.enter_context(nc.psum_tensor("ring", [P, 4, S], F32))
        nat = ctx.enter_context(nc.psum_tensor("nat", [P, 2, S], F32))
        bank_m = ctx.enter_context(nc.psum_tensor("bank_m", [P, S], F32))
        bank_y = ctx.enter_context(nc.psum_tensor("bank_y", [P, S], F32))

        q_dram = nc.dram_tensor("q_dram", [2, TERMS, DH, PAIRS, S], BF16, kind="Internal").ap()
        k_dram = nc.dram_tensor("k_dram", [2, TERMS, DH, PAIRS, S], BF16, kind="Internal").ap()
        m_dram = nc.dram_tensor("m_dram", [3, 2, PAIRS, S], BF16, kind="Internal").ap()
        c_dram = nc.dram_tensor("c_dram", [NE, S], F32, kind="Internal").ap()

        x_loaded = [sem(f"x_loaded{n}") for n in range(4)]
        w_loaded = sem("w_loaded")
        small_loaded = sem("small_loaded")
        ones_set = sem("ones_set")
        const_made = sem("const_made")
        wd_loaded = sem("wd_loaded")
        w_hi_done = sem("w_hi_done")
        w_lo_done = sem("w_lo_done")
        ln_step = sem("ln_step")
        sqrt_done = sem("sqrt_done")

        xn_done = sem("xn_done")
        xT_ready = sem("xT_ready")
        xnT_done = sem("xnT_done")
        xhl_step = sem("xhl_step")
        q_ready = sem("q_ready")
        k_ready = sem("k_ready")
        v_ready = sem("v_ready")
        q_done = sem("q_done")
        k_done = sem("k_done")
        v_done = sem("v_done")
        v_placed = sem("v_placed")
        qsplit_step = sem("qsplit_step")
        ksplit_step = sem("ksplit_step")
        q_written = sem("q_written")
        k_written = sem("k_written")
        ops_loaded = [sem(f"ops_loaded{n}") for n in range(2)]
        logits_ready = sem("logits_ready")
        router_exp = sem("router_exp")
        router_step = sem("router_step")
        combT_ready = sem("combT_ready")
        combT_done = sem("combT_done")
        comb_written = sem("comb_written")
        cb_loaded = sem("cb_loaded")
        cb_others = sem("cb_others")

        gate_ready = sem("gate_ready")
        up_ready = sem("up_ready")
        silu_done = sem("silu_done")
        weighted = sem("weighted")
        hid_done = sem("hid_done")
        down_done = sem("down_done")
        y_taken = sem("y_taken")
        yback_ready = sem("yback_ready")
        base_done = sem("base_done")

        nat_ready = sem("nat_ready")
        nat_max = sem("nat_max")
        msplit_step = sem("msplit_step")
        mT_ready = sem("mT_ready")
        mrows_done = sem("mrows_done")
        m_written = sem("m_written")
        m_loaded = sem("m_loaded")

        st_ready = sem("st_ready")
        exp_done = sem("exp_done")
        masked = sem("masked")
        pv_done = sem("pv_done")
        o_taken = sem("o_taken")
        oback_ready = sem("oback_ready")
        rden_done = sem("rden_done")
        o_normed = sem("o_normed")
        onT_ready = sem("onT_ready")
        onT_done = sem("onT_done")
        proj_ready = sem("proj_ready")
        tail_step = sem("tail_step")
        summed = sem("summed")
        stored = sem("stored")

        pe_passed = sem("pe_passed")
        dve_passed = sem("dve_passed")
        pool_passed = sem("pool_passed")
        sp_passed = sem("sp_passed")

        NAT_ALL = NAT * GROUPS
        ST_ALL = UNITS * GROUPS
        FIRST_SEGMENTS = [s for s in expert_segments() if s[0] < EARLY]
        OTHER_SEGMENTS = [s for s in expert_segments() if s[0] >= EARLY]
        OP_LOADS = 4
        PART_WRITES = 6
        XT = NB * QT // 4
        LN_STEPS = 12
        LN_PARTS = [slice(0, XT), slice(XT, 4 * XT)]
        ROUTER_STEPS = 15

        def half(h):
            return HALF * (h % 2)

        def apart(eng, counter):
            eng.sem_inc(counter, 1)

        def before(eng, s, count):
            if not (isinstance(count, int) and count == 0):
                eng.wait_ge(s, count)

        block = ctx.enter_context(nc.Block())

        @block.sync
        def _(sp):
            def tokens_in(n):
                sp.dma_start(x_sb[:, n * XT:(n + 1) * XT, :],
                             x.rearrange("b (q p) e -> p (b q) e", p=P)[:, n * XT:(n + 1) * XT, :]
                             ).then_inc(x_loaded[n], 16)

            tokens_in(0)
            small = [(ident_sb[:, :], ident), (wqk_sb[:, :, :], wqkT), (wv_sb[:, :], wvT),
                     (bqk[:, :], b_qk), (bv_bc[:, :], b_v.partition_broadcast(P)),
                     (gate_sb[:, :], gateT), (halfid_f[:, :, :], halfid),
                     (mask_f[:, :, 0, :], halfmask), (mask_f[:, :, 1, :], halfmask),
                     (lower_sb[:, :, :], lower.partition_broadcast(P)),
                     (wo_sb[:, :], woT), (bo_bc[:, :], b_o.partition_broadcast(P))]
            for dst, src in small:
                sp.dma_start(dst, src).then_inc(small_loaded, 16)
            tokens_in(1)
            tokens_in(2)
            tokens_in(3)
            sp.dma_start(w_raw, w_gu).then_inc(w_loaded, 16)
            sp.dma_start(wd_sb[:, 0:NT - 1, :], w_dn[0:(NT - 1) * P, :].rearrange("(t p) e -> p t e", p=P)
                         ).then_inc(wd_loaded, 16)
            sp.dma_start(wd_sb[0:LAST, NT - 1, :], w_dn[(NT - 1) * P:FT, :]).then_inc(wd_loaded, 16)

            def k_parts_out(j):
                sp.wait_ge(ksplit_step, 4 * j + 4)
                for s in range(2):
                    own = k_parts[HALF * s:HALF * (s + 1), :, :]
                    for first, n in ((0, 3), (3, 2), (5, 1)):
                        sp.dma_start(k_dram[s, first:first + n].rearrange("t d i n -> (d i) t n"),
                                     own[:, 0:n, :]).then_inc(k_written, 16)

            def q_parts_out(j):
                sp.wait_ge(qsplit_step, 4 * j + 4)
                for s in range(2):
                    own = q_parts[HALF * s:HALF * (s + 1), :, :]
                    for first, n, part in ((0, 3, 0), (3, 2, 1), (5, 1, 2)):
                        sp.dma_start(q_dram[s, first:first + n].rearrange("t d i n -> (d i) t n"),
                                     own[:, part:part + 1, :].to_broadcast([HALF, n, S])
                                     ).then_inc(q_written, 16)

            def weights_out(j):
                sp.wait_ge(combT_done, j + 1)
                sp.dma_start(c_dram, combT[:, :]).then_inc(comb_written, 16)
                sp.wait_ge(comb_written, 16 * j + 16)

            def weights_around(segments, loaded):
                for t, p0, n, e in segments:
                    sp.dma_start(cb[p0:p0 + n, t, :], c_dram[e, :].partition_broadcast(n)).then_inc(loaded, 16)

            def operands_in(j, i):
                sp.wait_ge(q_written, PART_WRITES * 16 * (j + 1))
                sp.wait_ge(k_written, PART_WRITES * 16 * (j + 1))
                for n in range(2):
                    if i is not None:
                        sp.wait_ge(st_ready, ST_ALL * i + ST_ALL * (n + 1) // 2)
                    apart(sp, sp_passed)
                    own = slice(n * PAIRS // 2, (n + 1) * PAIRS // 2)
                    for s in range(2):
                        rows = slice(HALF * s, HALF * s + SROWS)
                        sp.dma_start(q_op[rows, own, :], q_dram[s, :, :, own, :].rearrange("t d i n -> (t d) i n")
                                     ).then_inc(ops_loaded[n], 16)
                        sp.dma_start(k_op[rows, own, :], k_dram[s, :, :, own, :].rearrange("t d i n -> (t d) i n")
                                     ).then_inc(ops_loaded[n], 16)

            def store(i):
                sp.wait_ge(tail_step, 3 * i + 3)
                sp.dma_start(out[i].rearrange("(q p) e -> p q e", p=P), base[:, :, :]).then_inc(stored, 16)

            def maxima_in(b):
                sp.wait_ge(mrows_done, b + 1)
                before(sp, stored, 16 * b)
                sp.dma_start(m_dram.rearrange("a s i n -> (a s i) n"), max_rows[:, :]).then_inc(m_written, 16)
                sp.wait_ge(m_written, 16 * b + 16)
                for s in range(2):
                    row = HALF * s + SROWS
                    sp.dma_start(q_op[row:row + MROWS, :, :], m_dram[:, s, :, :]).then_inc(m_loaded, 16)

            q_parts_out(0)
            k_parts_out(0)
            weights_out(0)
            weights_around(FIRST_SEGMENTS, cb_loaded)
            sp.wait_ge(ones_set, 1)
            operands_in(0, None)
            weights_around(OTHER_SEGMENTS, cb_others)
            maxima_in(0)
            with sp.Fori(0, NB - 1) as i:
                k_parts_out(i + 1)
                q_parts_out(i + 1)
                weights_out(i + 1)
                weights_around(FIRST_SEGMENTS, cb_loaded)
                operands_in(i + 1, i)
                weights_around(OTHER_SEGMENTS, cb_others)
                store(i)
                maxima_in(i + 1)
            store(NB - 1)
            sp.wait_ge(stored, 16 * NB)

        @block.tensor
        def _(pe):
            def transpose_x(j):
                pe.wait_ge(xn_done, j + 1)
                before(pe, nat_max, NAT_ALL * j)
                for q in range(QT):
                    mm = pe.transpose(nat[:, 0, q * P:(q + 1) * P], xn[:, q, :], ident_sb[:, :])
                mm.then_inc(xT_ready, 1)

            def project_k(j):
                pe.wait_ge(xnT_done, j + 1)
                pe.matmul(nat[:, 1, :], wqk_sb[:, 1, :], xnT[:, :], start=True, stop=True).then_inc(k_ready, 1)

            def project_q(j):
                pe.wait_ge(xnT_done, j + 1)
                pe.matmul(nat[:, 0, :], wqk_sb[:, 0, :], xnT[:, :], start=True, stop=True).then_inc(q_ready, 1)

            def project_v(j):
                before(pe, base_done, j)
                for q in range(QT):
                    mm = pe.matmul(bank_m[:, q * P:(q + 1) * P], xnT[:, q * P:(q + 1) * P], wv_sb[:, :],
                                   start=True, stop=True)
                mm.then_inc(v_ready, 1)

            def logits(j):
                pe.wait_ge(xnT_done, j + 1)
                before(pe, y_taken, j)
                for q in range(QT):
                    mm = pe.matmul(bank_y[:, q * NE:(q + 1) * NE], xnT[:, q * P:(q + 1) * P], gate_sb[:, :],
                                   start=True, stop=True)
                mm.then_inc(logits_ready, 1)

            def transpose_comb(j):
                pe.wait_ge(router_step, ROUTER_STEPS * j + ROUTER_STEPS)
                pe.wait_ge(v_done, j + 1)
                for q in range(QT):
                    mm = pe.transpose(bank_m[0:NE, q * P:(q + 1) * P], comb[:, q, :], ident_sb[:, :])
                mm.then_inc(combT_ready, 1)

            def gate_up(b, k):
                tile = TILE_ORDER[k]
                n = rows_of(tile)
                if k == 0:
                    pe.wait_ge(xhl_step, 2 * b + 2)
                if k < 2 and not (isinstance(b, int) and b == 0):
                    pe.wait_ge(exp_done, ST_ALL * b - 1 + k)
                if k >= 2:
                    pe.wait_ge(hid_done, NT * b + k - 1)
                for w, ready in ((0, gate_ready), (1, up_ready)):
                    bank = ring[0:n, 2 * (k % 2) + w, :]
                    cols = slice(tile * P, tile * P + n)
                    pe.matmul(bank, w_hi[:, w, cols], x_hi[:, :], start=True, stop=False)
                    pe.matmul(bank, w_hi[:, w, cols], x_lo[:, :], start=False, stop=False)
                    pe.matmul(bank, w_lo[:, w, cols], x_hi[:, :], start=False, stop=True).then_inc(ready, 1)

            def down(b, k, i):
                tile = TILE_ORDER[k]
                n = rows_of(tile)
                pe.wait_ge(hid_done, NT * b + k + 1)
                if k == 0:
                    pe.wait_ge(router_step, ROUTER_STEPS * b + 2)
                    if i is not None:
                        pe.wait_ge(o_normed, GROUPS * i + 3)
                pe.matmul(bank_y[:, :], wd_sb[0:n, tile, :], hid[0:n, k % 3, :],
                          start=(k == 0), stop=(k == NT - 1)).then_inc(down_done, 1)

            def mask_scores(bank, r, cols):
                c0, nblk, stride = cols
                for c in range(2):
                    w = P if c == 0 else HALF
                    if stride == P and nblk == 2 or nblk == 1:
                        o = bank[:, c0:c0 + nblk * P].rearrange("p (k n) -> p k n", k=nblk)[:, :, P - w:P]
                    else:
                        o = bank.rearrange("p (k n) -> p k n", n=stride)[:, :, c0:c0 + P][:, :, P - w:P]
                    mm = pe.matmul(o, halfid_bf[r:r + HALF, c, :], mask_bf[r:r + HALF, c, 0:nblk, P - w:P],
                                   start=False, stop=(c == 1), skip_group_check=True)
                return mm

            def scores(b, g, u):
                n = NAT * g + u
                bank = nat[:, n % 2, :]
                if n in (0, NAT_ALL // 2):
                    pe.wait_ge(ops_loaded[n // (NAT_ALL // 2)], OP_LOADS * 16 * b + OP_LOADS * 16)
                if n == 0:
                    if isinstance(b, int) and b == 0:
                        pe.wait_ge(q_done, 1)
                        pe.wait_ge(k_done, 1)
                    else:
                        pe.wait_ge(o_taken, GROUPS * b)
                if n >= 2:
                    pe.wait_ge(nat_max, NAT_ALL * b + n - 1)
                if u < 8:
                    h = 4 * g + u % 4
                    r = half(h)
                    q = q_op[r:r + SROWS, h // 2, :]
                    k = k_op[r:r + SROWS, h // 2, :]
                    if u < 4:
                        pe.matmul(bank, q[:, 3 * P:4 * P], k, start=True, stop=False, skip_group_check=True)
                        mm = mask_scores(bank, r, (3 * P, 1, P))
                    else:
                        pe.matmul(bank[:, 0:3 * P], q[:, 2 * P:3 * P], k[:, 0:3 * P],
                                  start=True, stop=False, skip_group_check=True)
                        pe.matmul(bank[:, 3 * P:4 * P], q[:, 0:P], k[:, 0:P],
                                  start=False, stop=False, skip_group_check=True)
                        mm = mask_scores(bank, r, (2 * P, 2, P))
                else:
                    for n2, h in enumerate((4 * g + u - 8, 4 * g + u - 6)):
                        r = half(h)
                        pe.matmul(bank[:, n2 * 2 * P:(n2 + 1) * 2 * P], q_op[r:r + SROWS, h // 2, P:2 * P],
                                  k_op[r:r + SROWS, h // 2, 0:2 * P],
                                  start=(n2 == 0), stop=False, skip_group_check=True)
                    mm = mask_scores(bank, r, (P, 2, 2 * P))
                mm.then_inc(nat_ready, 1)

            def transpose_maxima(b):
                pe.wait_ge(msplit_step, 4 * b + 4)
                before(pe, tail_step, 3 * b)
                pe.wait_ge(combT_done, b + 1)
                apart(pe, pe_passed)
                rows = bank_m[0:3 * H, 0:S // 2].bitcast(BF16)
                for q in range(QT):
                    mm = pe.transpose(rows[:, q * P:(q + 1) * P],
                                      max_parts[:, q, :, :, :].rearrange("p a s i -> p (a s i)"), ident_bf[:, :])
                mm.then_inc(mT_ready, 1)

            def transpose_y(b):
                pe.wait_ge(y_taken, b + 1)
                pe.wait_ge(mrows_done, b + 1)
                for q in range(QT):
                    mm = pe.transpose(bank_m[:, q * P:(q + 1) * P], yT[:, q * P:(q + 1) * P], ident_sb[:, :])
                mm.then_inc(yback_ready, 1)

            def scores_t(i, g, u):
                n = UNITS * g + u
                if n == 0:
                    pe.wait_ge(m_loaded, 32 * i + 32)
                    pe.wait_ge(hid_done, NT * i + NT)
                elif n >= 2:
                    pe.wait_ge(exp_done, ST_ALL * i + n - 1)
                rows = SROWS + MROWS
                for a in range(2):
                    bank = ring[:, 2 * (n % 2) + a, :]
                    if u < 4:
                        h = 4 * g + 2 * (u % 2) + a
                        parts = [(h, 0, 0)] if u < 2 else [(h, 1, 0), (h, 3, 3 * P)]
                    else:
                        parts = [(4 * g + a, 2, 0), (4 * g + 2 + a, 2, 2 * P)]
                    for h, kb, at in parts:
                        r = half(h)
                        mm = pe.matmul(bank[:, at:at + S - kb * P],
                                       k_op[r:r + rows, h // 2, kb * P:(kb + 1) * P],
                                       q_op[r:r + rows, h // 2, kb * P:S], start=True, stop=True)
                mm.then_inc(st_ready, 1)

            def probs_of(g, j, kb):
                buf = probs[:, g % 2, :, :]
                if kb == 0:
                    return buf[:, j, :]
                if kb == 1:
                    return buf[:, 4 + j, 0:3 * P]
                if kb == 3:
                    return buf[:, 4 + j, 3 * P:4 * P]
                return buf[:, 8 + j % 2, (j // 2) * 2 * P:(j // 2 + 1) * 2 * P]

            def weigh_v(i, g, c, front):
                kb = KB_ORDER[c]
                pe.wait_ge(masked, 4 * GROUPS * i + 4 * g + c + 1)
                if c == 0:
                    if g == 0:
                        pe.wait_ge(v_placed, i + 1)
                    if g < 2 and front:
                        pe.wait_ge((q_done, k_done)[g], i + 2)
                    if g >= 2:
                        pe.wait_ge(o_taken, GROUPS * i + g - 1)
                for j in range(4):
                    mm = pe.matmul(nat[32 * j:32 * j + 32, g % 2, kb * P:S], v_op[:, kb, 4 * g + j, :],
                                   probs_of(g, j, kb), start=(c == 0), stop=(c == 3),
                                   tile_position=(0, 32 * j), skip_group_check=True)
                if c == 3:
                    mm.then_inc(pv_done, 1)

            def transpose_o(i, g, front):
                pe.wait_ge(o_taken, GROUPS * i + g + 1)
                bank = bank_y if g % 2 == 0 else bank_m
                if g == 0:
                    if front:
                        pe.wait_ge(router_step, ROUTER_STEPS * i + ROUTER_STEPS + 2)
                    else:
                        pe.wait_ge(y_taken, i + 1)
                elif g == 1:
                    if front:
                        pe.wait_ge(combT_done, i + 2)
                    else:
                        pe.wait_ge(base_done, i + 1)
                else:
                    pe.wait_ge(o_normed, GROUPS * i + g - 1)
                for q in range(QT):
                    mm = pe.transpose(bank[:, q * P:(q + 1) * P], o_sb[:, g % 2, q * P:(q + 1) * P],
                                      ident_sb[:, :])
                mm.then_inc(oback_ready, 1)

            def transpose_on(i):
                pe.wait_ge(o_normed, GROUPS * i + GROUPS)
                for q in range(QT):
                    mm = pe.transpose(bank_m[:, q * P:(q + 1) * P], o_norm[:, q, :], ident_sb[:, :])
                mm.then_inc(onT_ready, 1)

            def project_out(i):
                pe.wait_ge(onT_done, i + 1)
                for q in range(QT):
                    mm = pe.matmul(bank_m[:, q * P:(q + 1) * P], o_normT[:, q * P:(q + 1) * P], wo_sb[:, :],
                                   start=True, stop=True)
                mm.then_inc(proj_ready, 1)

            def experts_and_maxima(b, i, front):
                n = 0
                for k in range(NT + 2):
                    if k < NT and (k >= 2 or i is None):
                        gate_up(b, k)
                    if k == 0 and i is not None:
                        transpose_o(i, 3, True)
                    for part in range(2):
                        for _ in range(PAIRS_AT[k][part]):
                            scores(b, n // NAT, n % NAT)
                            scores(b, (n + 1) // NAT, (n + 1) % NAT)
                            n += 2
                        if part == 0 and k >= 2:
                            down(b, k - 2, i)
                    if k == 1 and i is not None:
                        transpose_on(i)
                    if k == 2 and i is not None:
                        project_out(i)
                    if k == 13:
                        transpose_maxima(b)
                        if front:
                            transpose_x(b + 1)
                    if k == 14 and front:
                        project_k(b + 1)
                if front:
                    project_q(b + 1)

            def attend(i, front):
                transpose_y(i)
                if front:
                    logits(i + 1)
                for g in range(GROUPS + 1):
                    for u in range(UNITS):
                        if g < GROUPS:
                            scores_t(i, g, u)
                        if front and g == GROUPS and u in (2, 3):
                            gate_up(i + 1, u - 2)
                        if g > 0 and u < 4:
                            weigh_v(i, g - 1, u, front)
                        if u == 2 and g in (2, 3, 4):
                            transpose_o(i, g - 2, front)
                        if front:
                            if (g, u) == (0, 1):
                                project_v(i + 1)
                            if (g, u) == (2, 0):
                                transpose_comb(i + 1)

            pe.wait_ge(small_loaded, 12 * 16)
            transpose_x(0)
            logits(0)
            project_q(0)
            project_k(0)
            project_v(0)
            transpose_comb(0)
            pe.wait_ge(const_made, 4)
            pe.wait_ge(w_lo_done, 2)
            pe.wait_ge(wd_loaded, 32)
            experts_and_maxima(0, None, True)
            with pe.Fori(0, NB - 2) as i:
                attend(i, True)
                experts_and_maxima(i + 1, i, True)
            attend(NB - 2, True)
            experts_and_maxima(NB - 1, NB - 2, False)
            attend(NB - 1, False)
            transpose_o(NB - 1, 3, False)
            transpose_on(NB - 1)
            project_out(NB - 1)

        @block.scalar
        def _(act):
            def square_root(part):
                act.wait_ge(ln_step, LN_STEPS * part + 7)
                nc.scalar.activation(ln[:, 5, LN_PARTS[part]], ln[:, 4, LN_PARTS[part]], ACT.Sqrt
                                     ).then_inc(sqrt_done, 1)

            def take_xT(j):
                act.wait_ge(xT_ready, j + 1)
                nc.scalar.activation(xnT[:, :], nat[:, 0, :], ACT.Copy).then_inc(xnT_done, 1)

            def take_q(j):
                act.wait_ge(q_ready, j + 1)
                nc.scalar.activation(qk_f[:, 0, :], nat[:, 0, :], ACT.Identity, bias=bq_scaled[:, 0:1],
                                     scale=QSCALE).then_inc(q_done, 1)

            def take_k(j):
                act.wait_ge(k_ready, j + 1)
                nc.scalar.activation(qk_f[:, 1, :], nat[:, 1, :], ACT.Identity, bias=bqk[:, 1:2],
                                     scale=1.0).then_inc(k_done, 1)

            def exp_router(j):
                act.wait_ge(router_step, ROUTER_STEPS * j + 2)
                nc.scalar.activation(rt[:, 1, :, :], rt[:, 0, :, :], ACT.Exp).then_inc(router_exp, 1)

            def silu(b, k):
                n = rows_of(TILE_ORDER[k])
                act.wait_ge(gate_ready, NT * b + k + 1)
                if k >= 3:
                    act.wait_ge(hid_done, NT * b + k - 2)
                else:
                    before(act, hid_done, NT * b)
                nc.scalar.activation(sg[0:n, k % 3, :], ring[0:n, 2 * (k % 2), :], ACT.Silu
                                     ).then_inc(silu_done, 1)

            def experts(b, i, front):
                for k in range(NT):
                    silu(b, k)
                    if k == 1 and i is not None:
                        act.wait_ge(onT_ready, i + 1)
                        nc.scalar.activation(o_normT[:, :], bank_m[:, :], ACT.Copy).then_inc(onT_done, 1)
                    if k == 13:
                        act.wait_ge(mT_ready, b + 1)
                        nc.scalar.activation(max_rows[:, :], bank_m[0:3 * H, 0:S // 2].bitcast(BF16), ACT.Copy
                                             ).then_inc(mrows_done, 1)
                if front:
                    take_xT(b + 1)
                    take_k(b + 1)
                act.wait_ge(down_done, NT * b + NT)
                nc.scalar.activation(yT[:, :], bank_y[:, :], ACT.Copy).then_inc(y_taken, 1)
                if front:
                    take_q(b + 1)
                nc.scalar.activation(table_call[:, :], bqk[:, 1:2], ACT.Exp)

            def attend(i, front):
                for g in range(GROUPS):
                    for u in range(UNITS):
                        n = UNITS * g + u
                        act.wait_ge(st_ready, ST_ALL * i + n + 1)
                        if u == 0 and g >= 2:
                            act.wait_ge(pv_done, GROUPS * i + g - 1)
                        nc.scalar.activation(probs[:, g % 2, 2 * u:2 * u + 2, :],
                                             ring[:, 2 * (n % 2):2 * (n % 2) + 2, :], ACT.Exp
                                             ).then_inc(exp_done, 1)
                        if front:
                            if (g, u) == (0, 1):
                                exp_router(i + 1)

            def high_weights(w):
                nc.scalar.activation(w_hi[:, w, :], w_raw[:, w, :], ACT.Copy).then_inc(w_hi_done, 1)

            square_root(0)
            take_xT(0)
            act.wait_ge(const_made, 1)
            take_q(0)
            take_k(0)
            square_root(1)
            exp_router(0)
            act.wait_ge(w_loaded, 16)
            high_weights(0)
            high_weights(1)
            act.wait_ge(w_lo_done, 2)
            experts(0, None, True)
            with act.Fori(0, NB - 2) as i:
                attend(i, True)
                experts(i + 1, i, True)
            attend(NB - 2, True)
            experts(NB - 1, NB - 2, False)
            attend(NB - 1, False)
            act.wait_ge(onT_ready, NB)
            nc.scalar.activation(o_normT[:, :], bank_m[:, :], ACT.Copy).then_inc(onT_done, 1)

        @block.gpsimd
        def _(pool):
            nc.gpsimd.memset(k_op[:, :, :], 1.0).then_inc(ones_set, 1)
            nc.gpsimd.memset(v_op[:, :, :, DH + 1:32], 0.0)
            nc.gpsimd.memset(v_op[:, :, :, DH:DH + 1], 1.0)

            def place_v(j, i):
                pool.wait_ge(v_done, j + 1)
                if i is not None:
                    pool.wait_ge(pv_done, GROUPS * i + GROUPS)
                apart(pool, pool_passed)
                nc.gpsimd.tensor_copy(v_op[:, :, :, 0:DH], v_new[:, :, :].rearrange(
                    "p q (h d) -> p q h d", h=H)).then_inc(v_placed, 1)

            def weigh_hidden(b, k):
                pool.wait_ge(silu_done, NT * b + k + 1)
                nc.gpsimd.tensor_tensor(sg[:, k % 3, :], sg[:, k % 3, :], cb[:, TILE_ORDER[k], :], ALU.mult
                                        ).then_inc(weighted, 1)

            def experts(b, i):
                pool.wait_ge(cb_loaded, 16 * len(FIRST_SEGMENTS) * (b + 1))
                for k in range(NT - ROUTED, NT):
                    if k == NT - ROUTED + 1 and i is not None:
                        sum_all(i)
                    if k == NT - ROUTED + EARLY:
                        pool.wait_ge(cb_others, 16 * len(OTHER_SEGMENTS) * (b + 1))
                    weigh_hidden(b, k)

            def sum_all(i):
                pool.wait_ge(tail_step, 3 * i + 1)
                nc.gpsimd.tensor_tensor(both[:, :, :], att[:, :, :], base[:, :, :], ALU.add).then_inc(summed, 1)

            def mask(view):
                apart(pool, pool_passed)
                return nc.gpsimd.affine_select(out=view, in_=view, compare_op=ALU.is_ge, fill=0.0, base=0,
                                               pattern=[[0, 4], [1, P]], channel_multiplier=-1)

            def attend(i, front):
                for g in range(GROUPS):
                    buf = probs[:, g % 2, :, :]
                    first = ST_ALL * i + UNITS * g
                    pool.wait_ge(exp_done, first + 2)
                    mask(buf[:, 0:4, 0:P]).then_inc(masked, 1)
                    pool.wait_ge(exp_done, first + 4)
                    mask(buf[:, 4:8, 0:P]).then_inc(masked, 1)
                    mask(buf[:, 4:8, 3 * P:4 * P]).then_inc(masked, 1)
                    pool.wait_ge(exp_done, first + 5)
                    mask(buf[:, 8:10, :].rearrange("p b (j n) -> p (b j) n", j=2)[:, :, 0:P]
                         ).then_inc(masked, 1)
                if front:
                    place_v(i + 1, i)

            pool.wait_ge(w_hi_done, 1)
            nc.gpsimd.tensor_tensor(w_lo[:, 0, :], w_raw[:, 0, :], w_hi[:, 0, :].bitcast(F32),
                                    ALU.subtract).then_inc(w_lo_done, 1)
            place_v(0, None)
            experts(0, None)
            with pool.Fori(0, NB - 2) as i:
                attend(i, True)
                experts(i + 1, i)
            attend(NB - 2, True)
            experts(NB - 1, NB - 2)
            attend(NB - 1, False)
            sum_all(NB - 1)

        @block.vector
        def _(dve):
            def statistics(n):
                dve.wait_ge(x_loaded[n], 16)
                for t in range(n * XT, (n + 1) * XT):
                    last = nc.vector.bn_stats(stats[:, t, :], x_sb[:, t, :])
                if n in (0, 3):
                    last.then_inc(ln_step, 1)

            def ln_rows(part, step):
                n = [step]

                def then(ins, wait=True):
                    n[0] += 1
                    ins.then_inc(ln_step, 1)
                    if wait:
                        dve.wait_ge(ln_step, LN_STEPS * part + n[0])

                return [ln[:, r, LN_PARTS[part]] for r in range(8)], then

            def mean_and_variance(part):
                v = nc.vector
                own = LN_PARTS[part]
                row, then = ln_rows(part, 1)
                dve.wait_ge(ln_step, LN_STEPS * part + 1)
                v.tensor_tensor(row[0], stats[:, own, 1], stats[:, own, 4], ALU.add)
                then(v.tensor_tensor(row[1], stats[:, own, 1], stats[:, own, 4], ALU.subtract))
                then(v.tensor_tensor(row[2], stats[:, own, 2], stats[:, own, 5], ALU.add), wait=False)
                then(v.scalar_tensor_tensor(out=row[3], in0=row[1], scalar=0.25, in1=row[1],
                                            op0=ALU.mult, op1=ALU.mult))
                then(v.tensor_scalar(row[2], row[2], 1.0 / E, EPS, ALU.mult, ALU.add))
                then(v.tensor_tensor(row[4], row[2], row[3], ALU.add), wait=False)
                then(v.tensor_scalar(row[0], row[0], 0.5, None, ALU.mult))

            def reciprocal_root(part):
                v = nc.vector
                row, then = ln_rows(part, 7)
                dve.wait_ge(sqrt_done, part + 1)
                then(v.reciprocal(row[6], row[5]))
                then(v.tensor_tensor(row[7], row[6], row[6], ALU.mult))
                then(v.tensor_tensor(row[7], row[7], row[4], ALU.mult))
                then(v.tensor_scalar(row[7], row[7], -0.5, 1.5, ALU.mult, ALU.add))
                then(v.tensor_tensor(row[6], row[6], row[7], ALU.mult))

            def normalise(j):
                before(dve, xT_ready, j)
                for q in range(QT):
                    at = bass.ds(j * QT + q, 1)
                    last = nc.vector.tensor_scalar(xn[:, q, :], x_sb[:, at, :].rearrange("p t e -> p (t e)"),
                                                   ln[:, 0, at], ln[:, 6, at], ALU.subtract, ALU.mult)
                last.then_inc(xn_done, 1)

            def split_x(j):
                dve.wait_ge(xnT_done, j + 1)
                if not (isinstance(j, int) and j == 0):
                    dve.wait_ge(up_ready, NT * j)
                nc.vector.tensor_copy(x_hi[:, :], xnT[:, :]).then_inc(xhl_step, 1)
                dve.wait_ge(xhl_step, 2 * j + 1)
                nc.vector.tensor_tensor(x_lo[:, :], xnT[:, :], x_hi[:, :].bitcast(F32), ALU.subtract
                                        ).then_inc(xhl_step, 1)

            def split_qk(j, n, taken, parts, step, written):
                whole, rest = qk_f[:, n, :], qk_rest[:, n, :]
                dve.wait_ge(taken, j + 1)
                before(dve, written, PART_WRITES * 16 * j)
                nc.vector.tensor_copy(parts[:, 0, :], whole).then_inc(step, 1)
                dve.wait_ge(step, 4 * j + 1)
                nc.vector.tensor_tensor(rest, whole, parts[:, 0, :], ALU.subtract).then_inc(step, 1)
                dve.wait_ge(step, 4 * j + 2)
                nc.vector.tensor_copy(parts[:, 1, :], rest).then_inc(step, 1)
                dve.wait_ge(step, 4 * j + 3)
                nc.vector.tensor_tensor(parts[:, 2, :], rest, parts[:, 1, :], ALU.subtract).then_inc(step, 1)

            def split_q(j):
                split_qk(j, 0, q_done, q_parts, qsplit_step, q_written)

            def split_k(j):
                split_qk(j, 1, k_done, k_parts, ksplit_step, k_written)

            def take_v(j):
                dve.wait_ge(v_ready, j + 1)
                before(dve, v_placed, j)
                nc.vector.tensor_tensor(v_new[:, :, :], bank_m[:, :].rearrange("p (q e) -> p q e", q=QT),
                                        bv_bc[:, :].unsqueeze(1).to_broadcast([P, QT, E]), ALU.add
                                        ).then_inc(v_done, 1)

            def wide(ap):
                return ap.unsqueeze(2).to_broadcast([P, QT, NE])

            def router_logits(j):
                lg = bank_y[:, 0:QT * NE].rearrange("p (q e) -> p q e", q=QT)
                dve.wait_ge(logits_ready, j + 1)
                nc.vector.reduce_max(rt_s[:, 0, :], lg, AX.X).then_inc(router_step, 1)
                dve.wait_ge(router_step, ROUTER_STEPS * j + 1)
                nc.vector.tensor_tensor(rt[:, 0, :, :], lg, wide(rt_s[:, 0, :]), ALU.subtract
                                        ).then_inc(router_step, 1)

            def router_weights(j):
                n = [2]

                def then(ins):
                    n[0] += 1
                    ins.then_inc(router_step, 1)
                    dve.wait_ge(router_step, ROUTER_STEPS * j + n[0])

                v = nc.vector
                score = rt[:, 2, :, :]
                of_e = score.unsqueeze(3).to_broadcast([P, QT, NE, NE])
                of_o = score.unsqueeze(2).to_broadcast([P, QT, NE, NE])
                above, ties = rt_pair[:, 0, :, :, :], rt_pair[:, 1, :, :, :]
                dve.wait_ge(router_exp, j + 1)
                then(v.reduce_sum(rt_s[:, 1, :], rt[:, 1, :, :], AX.X))
                then(v.reciprocal(rt_s[:, 1, :], rt_s[:, 1, :]))
                then(v.tensor_tensor(score, rt[:, 1, :, :], wide(rt_s[:, 1, :]), ALU.mult))
                then(v.tensor_tensor(ties, of_o, of_e, ALU.is_equal))
                then(v.tensor_tensor(ties, ties, lower_sb[:, :, :].unsqueeze(1).to_broadcast([P, QT, NE, NE]),
                                     ALU.mult))
                then(v.tensor_tensor(above, of_o, of_e, ALU.is_gt))
                then(v.tensor_tensor(above, above, ties, ALU.add))
                then(v.reduce_sum(rt[:, 3, :, :], above, AX.X))
                then(v.scalar_tensor_tensor(out=rt[:, 3, :, :], in0=rt[:, 3, :, :], scalar=1.5, in1=score,
                                            op0=ALU.is_lt, op1=ALU.mult))
                then(v.reduce_sum(rt_s[:, 2, :], rt[:, 3, :, :], AX.X))
                then(v.tensor_scalar(rt_s[:, 3, :], rt_s[:, 2, :], 1e-20, None, ALU.add))
                then(v.reciprocal(rt_s[:, 4, :], rt_s[:, 3, :]))
                then(v.scalar_tensor_tensor(out=comb[:, :, :], in0=rt[:, 3, :, :], scalar=ROUTE_SCALE,
                                            in1=wide(rt_s[:, 4, :]), op0=ALU.mult, op1=ALU.mult))
                assert n[0] == ROUTER_STEPS

            def take_combT(j):
                dve.wait_ge(combT_ready, j + 1)
                before(dve, comb_written, 16 * j)
                nc.vector.tensor_copy(combT[:, :], bank_m[0:NE, :]).then_inc(combT_done, 1)

            def hidden(b, k):
                n = rows_of(TILE_ORDER[k])
                shared = NT - ROUTED
                if k < shared:
                    dve.wait_ge(silu_done, NT * b + k + 1)
                else:
                    dve.wait_ge(weighted, ROUTED * b + k - shared + 1)
                dve.wait_ge(up_ready, NT * b + k + 1)
                before(dve, down_done, NT * b + (k - 2 if k >= 3 else 0))
                nc.vector.tensor_tensor(hid[0:n, k % 3, :], sg[0:n, k % 3, :], ring[0:n, 2 * (k % 2) + 1, :],
                                        ALU.mult).then_inc(hid_done, 1)

            def maxima(b, g, u):
                n = NAT * g + u
                bank = nat[:, n % 2, :]
                dve.wait_ge(nat_ready, NAT_ALL * b + n + 1)
                def neg(out, in_):
                    return nc.vector.tensor_reduce(out, in_, AX.X, ALU.max, negate=True)

                if u < 8:
                    h = 4 * g + u % 4
                    s, i = h % 2, h // 2
                if u < 4:
                    last = neg(neg_max[:, 3, s, i:i + 1], bank)
                elif u < 8:
                    neg(neg_max[:, 2, s, i:i + 1], bank[:, 0:3 * P])
                    last = neg(neg_max[:, 0, s, i:i + 1], bank[:, 3 * P:4 * P])
                else:
                    last = neg(neg_max[:, 1, u - 8, 2 * g:2 * g + 2], bank.rearrange("p (k n) -> p k n", k=2))
                last.then_inc(nat_max, 1)

            def split_maxima(b):
                dve.wait_ge(nat_max, NAT_ALL * b + NAT_ALL)
                before(dve, mT_ready, b)
                nc.vector.tensor_copy(max_parts[:, :, 0, :, :], neg_max[:, :, :, :]).then_inc(msplit_step, 1)
                dve.wait_ge(msplit_step, 4 * b + 1)
                nc.vector.tensor_tensor(max_rest[:, :, :, :], neg_max[:, :, :, :], max_parts[:, :, 0, :, :],
                                        ALU.subtract).then_inc(msplit_step, 1)
                dve.wait_ge(msplit_step, 4 * b + 2)
                nc.vector.tensor_copy(max_parts[:, :, 1, :, :], max_rest[:, :, :, :]).then_inc(msplit_step, 1)
                dve.wait_ge(msplit_step, 4 * b + 3)
                nc.vector.tensor_tensor(max_parts[:, :, 2, :, :], max_rest[:, :, :, :],
                                        max_parts[:, :, 1, :, :], ALU.subtract).then_inc(msplit_step, 1)

            def take_o(i, g):
                dve.wait_ge(pv_done, GROUPS * i + g + 1)
                if g >= 2:
                    dve.wait_ge(oback_ready, GROUPS * i + g - 1)
                nc.vector.tensor_copy(o_sb[:, g % 2, :], nat[:, g % 2, :]).then_inc(o_taken, 1)

            def normalise_o(i, g):
                bank = (bank_y if g % 2 == 0 else bank_m)[:, :].rearrange("p (q j c) -> p q j c", q=QT, j=4)
                dve.wait_ge(oback_ready, GROUPS * i + g + 1)
                nc.vector.reciprocal(o_rden[:, :, :, :], bank[:, :, :, DH:DH + 1]).then_inc(rden_done, 1)
                dve.wait_ge(rden_done, GROUPS * i + g + 1)
                nc.vector.tensor_tensor(
                    o_norm[:, :, 4 * DH * g:4 * DH * (g + 1)].rearrange("p q (j d) -> p q j d", j=4),
                    bank[:, :, :, 0:DH], o_rden[:, :, :, :].to_broadcast([P, QT, 4, DH]), ALU.mult
                ).then_inc(o_normed, 1)

            def add_tokens(b):
                dve.wait_ge(m_written, 16 * b + 16)
                dve.wait_ge(yback_ready, b + 1)
                nc.vector.tensor_tensor(base[:, :, :], bank_m[:, :].rearrange("p (q e) -> p q e", q=QT),
                                        x_sb[:, bass.ds(b * QT, QT), :], ALU.add).then_inc(base_done, 1)

            def add_attention(i):
                dve.wait_ge(proj_ready, i + 1)
                nc.vector.tensor_tensor(att[:, :, :], bank_m[:, :].rearrange("p (q e) -> p q e", q=QT),
                                        bo_bc[:, :].unsqueeze(1).to_broadcast([P, QT, E]), ALU.add
                                        ).then_inc(tail_step, 1)

            def find_numbers(i):
                dve.wait_ge(tail_step, 3 * i + 1)
                nc.vector.tensor_tensor(not_nan[:, :, :], att[:, :, :], att[:, :, :], ALU.is_equal
                                        ).then_inc(tail_step, 1)

            def finish_output(i):
                dve.wait_ge(tail_step, 3 * i + 2)
                apart(dve, dve_passed)
                dve.wait_ge(summed, i + 1)
                apart(dve, dve_passed)
                apart(dve, dve_passed)
                nc.vector.copy_predicated(base[:, :, :], not_nan[:, :, :], both[:, :, :]).then_inc(tail_step, 1)

            def experts_and_maxima(b, i, front):
                if i is not None:
                    take_o(i, 3)
                n = 0
                for k in range(NT + 1):
                    if k == 1 and i is not None:
                        normalise_o(i, 3)
                    if k >= 1:
                        hidden(b, k - 1)
                    for _ in range(sum(PAIRS_AT[k])):
                        maxima(b, n // NAT, n % NAT)
                        maxima(b, (n + 1) // NAT, (n + 1) % NAT)
                        n += 2
                    if k == 10 and front:
                        normalise(b + 1)
                    if k == 12:
                        split_maxima(b)
                    if k == 3 and i is not None:
                        add_attention(i)
                    if k == 5 and i is not None:
                        find_numbers(i)
                    if k == 7 and i is not None:
                        finish_output(i)

            def attend(i, front):
                add_tokens(i)
                if front:
                    router_logits(i + 1)
                    split_k(i + 1)
                    take_v(i + 1)
                    router_weights(i + 1)
                take_o(i, 0)
                if front:
                    split_q(i + 1)
                    take_combT(i + 1)
                normalise_o(i, 0)
                take_o(i, 1)
                if front:
                    split_x(i + 1)
                normalise_o(i, 1)
                take_o(i, 2)
                normalise_o(i, 2)

            statistics(0)
            mean_and_variance(0)
            reciprocal_root(0)
            normalise(0)
            dve.wait_ge(small_loaded, 12 * 16)
            nc.vector.tensor_scalar(bq_scaled[:, :], bqk[:, 0:1], QSCALE, None, ALU.mult).then_inc(const_made, 1)
            nc.vector.tensor_copy(ident_bf[:, :], ident_sb[:, :]).then_inc(const_made, 1)
            nc.vector.tensor_copy(halfid_bf[:, :, :], halfid_f[:, :, :]).then_inc(const_made, 1)
            nc.vector.tensor_copy(mask_bf[:, :, :, :], mask_f[:, :, :, :]).then_inc(const_made, 1)
            statistics(1)
            router_logits(0)
            statistics(2)
            statistics(3)
            mean_and_variance(1)
            split_q(0)
            split_k(0)
            take_v(0)
            router_weights(0)
            split_x(0)
            take_combT(0)
            dve.wait_ge(w_hi_done, 2)
            nc.vector.tensor_tensor(w_lo[:, 1, :], w_raw[:, 1, :], w_hi[:, 1, :].bitcast(F32),
                                    ALU.subtract).then_inc(w_lo_done, 1)
            reciprocal_root(1)
            experts_and_maxima(0, None, True)
            with dve.Fori(0, NB - 2) as i:
                attend(i, True)
                experts_and_maxima(i + 1, i, True)
            attend(NB - 2, True)
            experts_and_maxima(NB - 1, NB - 2, False)
            attend(NB - 1, False)
            take_o(NB - 1, 3)
            normalise_o(NB - 1, 3)
            add_attention(NB - 1)
            find_numbers(NB - 1)
            finish_output(NB - 1)


def kernel(L0_attn_x, L0_attn_w_in, L0_attn_b_in, L0_attn_w_out, L0_attn_b_out, L0_ffn_gate_w, L0_ffn_w_gate,
           L0_ffn_w_up, L0_ffn_w_down, L0_ffn_sw_gate, L0_ffn_sw_up, L0_ffn_sw_down):
    import numpy as np
    import concourse.bacc as bacc
    from concourse.bass_utils import run_bass_kernel_spmd

    def side_by_side(w, sw):
        return np.concatenate([np.transpose(w, (1, 0, 2)).reshape(E, NE * F), sw], axis=1)

    r = np.arange(P)
    halfid = np.zeros((P, 2, P), np.float32)
    halfmask = np.zeros((P, 2, P), np.float32)
    for c in range(2):
        q = HALF * c + r % HALF
        halfid[r, c, q] = 1.0
        halfmask[:, c, :] = np.where(r[None, :] > q[:, None], np.float32(-3e38), np.float32(0))
    lower = (np.arange(NE)[None, :] < np.arange(NE)[:, None]).astype(np.float32)

    w_in = np.asarray(L0_attn_w_in)
    b_in = np.asarray(L0_attn_b_in)
    ins = {
        "x": np.asarray(L0_attn_x),
        "wqkT": np.transpose(w_in[:2 * E].reshape(2, PAIRS, 2, DH, E), (4, 0, 2, 3, 1)).reshape(E, 2, E),
        "wvT": w_in[2 * E:].T,
        "b_qk": np.transpose(b_in[:2 * E].reshape(2, PAIRS, 2, DH), (2, 3, 1, 0)).reshape(E, 2),
        "b_v": b_in[2 * E:],
        "woT": np.asarray(L0_attn_w_out).T,
        "b_o": np.asarray(L0_attn_b_out),
        "gateT": np.asarray(L0_ffn_gate_w).T,
        "w_gu": np.stack([side_by_side(np.asarray(L0_ffn_w_gate), np.asarray(L0_ffn_sw_gate)),
                          side_by_side(np.asarray(L0_ffn_w_up), np.asarray(L0_ffn_sw_up))], axis=1),
        "w_dn": np.concatenate([np.asarray(L0_ffn_w_down).reshape(NE * F, E), np.asarray(L0_ffn_sw_down)]),
        "ident": np.eye(P, dtype=np.float32),
        "halfid": halfid,
        "halfmask": halfmask,
        "lower": lower,
    }
    nc = bacc.Bacc("TRN2", target_bir_lowering=False, num_devices=1)
    arrays, aps = {}, []
    for name, a in ins.items():
        a = np.ascontiguousarray(a)
        arrays[f"in_{name}"] = a
        aps.append(nc.dram_tensor(f"in_{name}", a.shape, mybir.dt.from_np(a.dtype), kind="ExternalInput").ap())
    out = nc.dram_tensor("out_0", (NB, S, E), F32, kind="ExternalOutput").ap()
    block_kernel(nc, *aps, out)
    res = run_bass_kernel_spmd(nc, [arrays], core_ids=[0])
    return res.results[0]["out_0"]
```
